# Optimizing a Trainium2 kernel written in Bass

```python
import numpy as np
import jax
import jax.numpy as jnp

def _softmax(x, axis=-1):
    return jax.nn.softmax(x, axis=axis)

def _gelu(x):
    return jax.nn.gelu(x, approximate=True)

def _silu(x):
    return jax.nn.silu(x)

def _sigmoid(x):
    return jax.nn.sigmoid(x)

def _layernorm(x, axis=-1, eps=1e-05):
    m = jnp.mean(x, axis=axis, keepdims=True)
    v = jnp.var(x, axis=axis, keepdims=True)
    return (x - m) / jnp.sqrt(v + eps)

def _scatter_add(tgt, idx, src, axis=0):
    return tgt.at[idx].add(src)

def _segment_sum(src, seg, n):
    return jax.ops.segment_sum(src, seg, n)
kernel_name = 'mk_xattn_seq_d2_seqx_r4_6cfafa'

def setup_inputs(seed: int=0):
    np.random.seed(seed)
    _w = jnp.asarray

    def _rec_inputs():
        import jax
        import jax.numpy as jnp
        _rk = jax.random.key(seed)
        x = -0.0002928 + 1 * jax.random.normal(jax.random.fold_in(_rk, 1), (16, 256, 512), jnp.float32)
        _lenS = 256 - jax.random.randint(jax.random.fold_in(_rk, 7), (16,), 0, max(1, 256 // 4) + 1, jnp.int32)
        _lenS2 = 256 - jax.random.randint(jax.random.fold_in(_rk, 8), (16,), 0, max(1, 256 // 4) + 1, jnp.int32)
        _ctx_2048P = jax.random.normal(jax.random.fold_in(_rk, 11), (16, 16, 512), jnp.float32)
        _ctx_2048c = jax.random.dirichlet(jax.random.fold_in(_rk, 511), 0.3 * jnp.ones((16,), jnp.float32), (16, 256))
        _ctx_2048t = jnp.einsum('bsk,bkd->bsd', _ctx_2048c, _ctx_2048P)
        _ctx_2048t = _ctx_2048t * jax.lax.rsqrt(jnp.mean(jnp.square(_ctx_2048t)) + 1e-12) * 0.953939
        ctx_2048 = -1.39393e-06 + 0.999914 * (_ctx_2048t + 0.3 * jax.random.normal(jax.random.fold_in(_rk, 611), (16, 256, 512), jnp.float32))
        _validS = jnp.arange(256)[None, :] < _lenS[:, None]
        _validS2 = jnp.arange(256)[None, :] < _lenS2[:, None]
        _causal = jnp.tril(jnp.ones((256, 256), dtype=bool))
        mask_1x1xSxS2_fc1 = jnp.where(jnp.broadcast_to(_validS2[0:1, None, None, :], (1, 1, 256, 256)), 1.0, 0.0).astype(jnp.float32)
        mask_Bx1xSxS2_ff1 = jnp.where(jnp.ones((16, 1, 256, 256), dtype=bool), 1.0, 0.0).astype(jnp.float32)
        return (x, ctx_2048, mask_1x1xSxS2_fc1, mask_Bx1xSxS2_ff1)
    x, ctx_2048, mask_1x1xSxS2_fc1, mask_Bx1xSxS2_ff1 = _rec_inputs()

    def _L0_xattn_setup():
        import jax, jax.numpy as jnp
        import numpy as np
        H = 512
        NH = 16
        HD = H // NH
        EPS = 1e-05

        def gelu(x):
            return 0.5 * x * (1.0 + jnp.tanh(0.7978845608028654 * x * (1.0 + 0.044715 * x * x)))

        def layernorm(x, scale, bias):
            m = jnp.mean(x, axis=-1, keepdims=True)
            v = jnp.mean(jnp.square(x - m), axis=-1, keepdims=True)
            return (x - m) * jax.lax.rsqrt(v + EPS) * scale + bias

        def split_heads(x):
            b, s, _ = x.shape
            return x.reshape(b, s, NH, HD).transpose(0, 2, 1, 3)

        def merge_heads(x):
            b, nh, s, hd = x.shape
            return x.transpose(0, 2, 1, 3).reshape(b, s, nh * hd)

        def attention(q, k, v, mask):
            scores = jnp.einsum('bhqd,bhkd->bhqk', q, k) / jnp.sqrt(jnp.float32(HD))
            scores = scores * mask - 10000.0 * (1.0 - mask)
            probs = jax.nn.softmax(scores, axis=-1)
            return jnp.einsum('bhqk,bhkd->bhqd', probs, v)
        key = jax.random.key(seed)
        ks = jax.random.split(key, 16)
        b, s, t = (2, 256, 256)
        w = lambda k, i, o: jax.random.normal(k, (i, o), jnp.float32) * 0.02
        inp = {'hidden_states': jax.random.normal(ks[0], (b, s, H), jnp.float32), 'encoder_states': jax.random.normal(ks[1], (b, t, H), jnp.float32), 'ltor_mask': jnp.tril(jnp.ones((1, 1, s, s), jnp.float32)), 'cross_mask': jnp.ones((b, 1, s, t), jnp.float32), 'ln1_s': jnp.ones((H,), jnp.float32), 'ln1_b': jnp.zeros((H,), jnp.float32), 'w_qkv': w(ks[2], H, 3 * H), 'b_qkv': jnp.zeros((3 * H,), jnp.float32), 'w_ao': w(ks[3], H, H), 'b_ao': jnp.zeros((H,), jnp.float32), 'ln2_s': jnp.ones((H,), jnp.float32), 'ln2_b': jnp.zeros((H,), jnp.float32), 'w_q': w(ks[4], H, H), 'b_q': jnp.zeros((H,), jnp.float32), 'w_kv': w(ks[5], H, 2 * H), 'b_kv': jnp.zeros((2 * H,), jnp.float32), 'w_co': w(ks[6], H, H), 'b_co': jnp.zeros((H,), jnp.float32), 'ln3_s': jnp.ones((H,), jnp.float32), 'ln3_b': jnp.zeros((H,), jnp.float32), 'w1': w(ks[7], H, 4 * H), 'b1': jnp.zeros((4 * H,), jnp.float32), 'w2': w(ks[8], 4 * H, H), 'b2': jnp.zeros((H,), jnp.float32)}
        return inp
    _L0_xattn_all = _L0_xattn_setup()
    _L0_xattn_in = {k: v for k, v in _L0_xattn_all.items() if k in ('ln1_s', 'ln1_b', 'w_qkv', 'b_qkv', 'w_ao', 'b_ao', 'ln2_s', 'ln2_b', 'w_q', 'b_q', 'w_kv', 'b_kv', 'w_co', 'b_co', 'ln3_s', 'ln3_b', 'w1', 'b1', 'w2', 'b2')}
    del _L0_xattn_all

    def _L1_xattn_setup():
        import jax, jax.numpy as jnp
        import numpy as np
        B, C, CI, N = (16, 256, 128, 512)
        EPS = 1e-05

        def _conv1x1(w, b, x):
            return jnp.einsum('oc,bcn->bon', w, x) + b[None, :, None]
        key = jax.random.key(seed)
        ks = jax.random.split(key, 14)
        s = 0.02
        return {'x': jax.random.normal(ks[0], (B, C, N), jnp.float32), 'x_2': jax.random.normal(ks[1], (B, C, N), jnp.float32), 'theta_w': jax.random.normal(ks[2], (CI, C), jnp.float32) * s, 'theta_b': jax.random.normal(ks[3], (CI,), jnp.float32) * s, 'phi_w': jax.random.normal(ks[4], (CI, C), jnp.float32) * s, 'phi_b': jax.random.normal(ks[5], (CI,), jnp.float32) * s, 'g_w': jax.random.normal(ks[6], (CI, C), jnp.float32) * s, 'g_b': jax.random.normal(ks[7], (CI,), jnp.float32) * s, 'w_w': jax.random.normal(ks[8], (C, CI), jnp.float32) * s, 'w_b': jax.random.normal(ks[9], (C,), jnp.float32) * s, 'bn_gamma': jax.random.normal(ks[10], (C,), jnp.float32), 'bn_beta': jax.random.normal(ks[11], (C,), jnp.float32), 'bn_mean': jax.random.normal(ks[12], (C,), jnp.float32), 'bn_var': jax.random.uniform(ks[13], (C,), jnp.float32, 0.5, 1.5)}
    _L1_xattn_all = _L1_xattn_setup()
    _L1_xattn_in = {k: v for k, v in _L1_xattn_all.items() if k in ('theta_w', 'theta_b', 'phi_w', 'phi_b', 'g_w', 'g_b', 'w_w', 'w_b', 'bn_gamma', 'bn_beta', 'bn_mean', 'bn_var')}
    del _L1_xattn_all
    return {'x': x, 'ctx_2048': ctx_2048, 'mask_1x1xSxS2_fc1': mask_1x1xSxS2_fc1, 'mask_Bx1xSxS2_ff1': mask_Bx1xSxS2_ff1, 'L0_xattn_ln1_s': _L0_xattn_in['ln1_s'], 'L0_xattn_ln1_b': _L0_xattn_in['ln1_b'], 'L0_xattn_w_qkv': _L0_xattn_in['w_qkv'], 'L0_xattn_b_qkv': _L0_xattn_in['b_qkv'], 'L0_xattn_w_ao': _L0_xattn_in['w_ao'], 'L0_xattn_b_ao': _L0_xattn_in['b_ao'], 'L0_xattn_ln2_s': _L0_xattn_in['ln2_s'], 'L0_xattn_ln2_b': _L0_xattn_in['ln2_b'], 'L0_xattn_w_q': _L0_xattn_in['w_q'], 'L0_xattn_b_q': _L0_xattn_in['b_q'], 'L0_xattn_w_kv': _L0_xattn_in['w_kv'], 'L0_xattn_b_kv': _L0_xattn_in['b_kv'], 'L0_xattn_w_co': _L0_xattn_in['w_co'], 'L0_xattn_b_co': _L0_xattn_in['b_co'], 'L0_xattn_ln3_s': _L0_xattn_in['ln3_s'], 'L0_xattn_ln3_b': _L0_xattn_in['ln3_b'], 'L0_xattn_w1': _L0_xattn_in['w1'], 'L0_xattn_b1': _L0_xattn_in['b1'], 'L0_xattn_w2': _L0_xattn_in['w2'], 'L0_xattn_b2': _L0_xattn_in['b2'], 'L1_xattn_theta_w': _L1_xattn_in['theta_w'], 'L1_xattn_theta_b': _L1_xattn_in['theta_b'], 'L1_xattn_phi_w': _L1_xattn_in['phi_w'], 'L1_xattn_phi_b': _L1_xattn_in['phi_b'], 'L1_xattn_g_w': _L1_xattn_in['g_w'], 'L1_xattn_g_b': _L1_xattn_in['g_b'], 'L1_xattn_w_w': _L1_xattn_in['w_w'], 'L1_xattn_w_b': _L1_xattn_in['w_b'], 'L1_xattn_bn_gamma': _L1_xattn_in['bn_gamma'], 'L1_xattn_bn_beta': _L1_xattn_in['bn_beta'], 'L1_xattn_bn_mean': _L1_xattn_in['bn_mean'], 'L1_xattn_bn_var': _L1_xattn_in['bn_var']}

def reference(x, ctx_2048, mask_1x1xSxS2_fc1, mask_Bx1xSxS2_ff1, L0_xattn_ln1_s, L0_xattn_ln1_b, L0_xattn_w_qkv, L0_xattn_b_qkv, L0_xattn_w_ao, L0_xattn_b_ao, L0_xattn_ln2_s, L0_xattn_ln2_b, L0_xattn_w_q, L0_xattn_b_q, L0_xattn_w_kv, L0_xattn_b_kv, L0_xattn_w_co, L0_xattn_b_co, L0_xattn_ln3_s, L0_xattn_ln3_b, L0_xattn_w1, L0_xattn_b1, L0_xattn_w2, L0_xattn_b2, L1_xattn_theta_w, L1_xattn_theta_b, L1_xattn_phi_w, L1_xattn_phi_b, L1_xattn_g_w, L1_xattn_g_b, L1_xattn_w_w, L1_xattn_w_b, L1_xattn_bn_gamma, L1_xattn_bn_beta, L1_xattn_bn_mean, L1_xattn_bn_var):
    import jax
    import jax.numpy as jnp

    def _L0_xattn_ref(hidden_states, encoder_states, ltor_mask, cross_mask, ln1_s, ln1_b, w_qkv, b_qkv, w_ao, b_ao, ln2_s, ln2_b, w_q, b_q, w_kv, b_kv, w_co, b_co, ln3_s, ln3_b, w1, b1, w2, b2):
        import jax, jax.numpy as jnp
        import numpy as np
        H = 512
        NH = 16
        HD = H // NH
        EPS = 1e-05

        def gelu(x):
            return 0.5 * x * (1.0 + jnp.tanh(0.7978845608028654 * x * (1.0 + 0.044715 * x * x)))

        def layernorm(x, scale, bias):
            m = jnp.mean(x, axis=-1, keepdims=True)
            v = jnp.mean(jnp.square(x - m), axis=-1, keepdims=True)
            return (x - m) * jax.lax.rsqrt(v + EPS) * scale + bias

        def split_heads(x):
            b, s, _ = x.shape
            return x.reshape(b, s, NH, HD).transpose(0, 2, 1, 3)

        def merge_heads(x):
            b, nh, s, hd = x.shape
            return x.transpose(0, 2, 1, 3).reshape(b, s, nh * hd)

        def attention(q, k, v, mask):
            scores = jnp.einsum('bhqd,bhkd->bhqk', q, k) / jnp.sqrt(jnp.float32(HD))
            scores = scores * mask - 10000.0 * (1.0 - mask)
            probs = jax.nn.softmax(scores, axis=-1)
            return jnp.einsum('bhqk,bhkd->bhqd', probs, v)
        ln_out = layernorm(hidden_states, ln1_s, ln1_b)
        qkv = ln_out @ w_qkv + b_qkv
        q, k, v = jnp.split(qkv, 3, axis=-1)
        ctx = merge_heads(attention(split_heads(q), split_heads(k), split_heads(v), ltor_mask))
        attn_out = ctx @ w_ao + b_ao
        x = hidden_states + attn_out
        ln_out = layernorm(x, ln2_s, ln2_b)
        q = ln_out @ w_q + b_q
        kv = encoder_states @ w_kv + b_kv
        k, v = jnp.split(kv, 2, axis=-1)
        ctx = merge_heads(attention(split_heads(q), split_heads(k), split_heads(v), cross_mask))
        cross_out = ctx @ w_co + b_co
        x = x + cross_out
        ln_out = layernorm(x, ln3_s, ln3_b)
        mlp_out = gelu(ln_out @ w1 + b1) @ w2 + b2
        return x + mlp_out

    def _L1_xattn_ref(x, x_2, theta_w, theta_b, phi_w, phi_b, g_w, g_b, w_w, w_b, bn_gamma, bn_beta, bn_mean, bn_var):
        import jax, jax.numpy as jnp
        import numpy as np
        B, C, CI, N = (16, 256, 128, 512)
        EPS = 1e-05

        def _conv1x1(w, b, x):
            return jnp.einsum('oc,bcn->bon', w, x) + b[None, :, None]
        g_x = _conv1x1(g_w, g_b, x_2).transpose(0, 2, 1)
        theta_x = _conv1x1(theta_w, theta_b, x).transpose(0, 2, 1)
        phi_x = _conv1x1(phi_w, phi_b, x_2)
        W = jnp.einsum('bnc,bcm->bnm', theta_x, phi_x) / phi_x.shape[-1]
        y = jnp.einsum('bnm,bmc->bnc', W, g_x).transpose(0, 2, 1)
        wy = _conv1x1(w_w, w_b, y)
        inv_std = jax.lax.rsqrt(bn_var + EPS)
        wy = bn_gamma[None, :, None] * (wy - bn_mean[None, :, None]) * inv_std[None, :, None] + bn_beta[None, :, None]
        return wy + x
    x = _L0_xattn_ref(x, ctx_2048, mask_1x1xSxS2_fc1, mask_Bx1xSxS2_ff1, L0_xattn_ln1_s, L0_xattn_ln1_b, L0_xattn_w_qkv, L0_xattn_b_qkv, L0_xattn_w_ao, L0_xattn_b_ao, L0_xattn_ln2_s, L0_xattn_ln2_b, L0_xattn_w_q, L0_xattn_b_q, L0_xattn_w_kv, L0_xattn_b_kv, L0_xattn_w_co, L0_xattn_b_co, L0_xattn_ln3_s, L0_xattn_ln3_b, L0_xattn_w1, L0_xattn_b1, L0_xattn_w2, L0_xattn_b2)
    x = _L1_xattn_ref(x, ctx_2048, L1_xattn_theta_w, L1_xattn_theta_b, L1_xattn_phi_w, L1_xattn_phi_b, L1_xattn_g_w, L1_xattn_g_b, L1_xattn_w_w, L1_xattn_w_b, L1_xattn_bn_gamma, L1_xattn_bn_beta, L1_xattn_bn_mean, L1_xattn_bn_var)
    return x

_drawn_inputs = setup_inputs


def setup_inputs(seed=0):
    import zlib

    import numpy as np

    out = dict(_drawn_inputs(seed))
    spreads = {'L0_xattn_ln1_s': (1.0, 0.6),
     'L0_xattn_ln1_b': (0.0, 0.686),
     'L0_xattn_b_qkv': (0.0, 0.303),
     'L0_xattn_b_ao': (0.0, 0.1),
     'L0_xattn_ln2_s': (1.0, 0.6),
     'L0_xattn_ln2_b': (0.0, 0.8),
     'L0_xattn_b_q': (0.0, 2.0),
     'L0_xattn_b_kv': (0.0, 0.297),
     'L0_xattn_b_co': (0.0, 0.1),
     'L0_xattn_ln3_s': (1.0, 0.556),
     'L0_xattn_ln3_b': (0.0, 0.553),
     'L0_xattn_b1': (0.0, 0.277),
     'L0_xattn_b2': (0.0, 0.1)}
    factors = {'L0_xattn_w_qkv': 3.956,
     'L0_xattn_w_q': 8.0,
     'L1_xattn_theta_w': 3.431,
     'L1_xattn_theta_b': 8.0,
     'L1_xattn_phi_w': 3.284,
     'L1_xattn_phi_b': 8.0,
     'L1_xattn_g_w': 3.473,
     'L1_xattn_g_b': 8.0,
     'L1_xattn_w_w': 3.22,
     'L1_xattn_w_b': 15.015}
    for name, (base, spread) in spreads.items():
        noise = np.random.default_rng([zlib.crc32(name.encode()), seed]).standard_normal(out[name].shape)
        drawn = base * np.exp(spread * noise) if base else spread * noise
        out[name] = jnp.asarray(drawn.astype(out[name].dtype))
    for name, factor in factors.items():
        out[name] = (out[name] * factor).astype(out[name].dtype)
    return out
```

```python
from contextlib import ExitStack

import numpy as np
import concourse.bass as bass
import concourse.mybir as mybir

F32 = mybir.dt.float32
F32R = mybir.dt.float32r
ALU = mybir.AluOpType
ACT = mybir.ActivationFunctionType

P = 128
B, S, H = 16, 256, 512
NH, HD = 16, 32
KT = H // P
TPB = S // P
BPB = 2
TOK = BPB * S
TT = TOK // P
NB = B // BPB
HPG = P // HD
NG = BPB * KT
FF = 4 * H
FT = FF // P
CI = 128
EPS = 1e-5
BIG = 3.0e38
DMA = 16


def wait(eng, sem, value):
    if isinstance(value, int) and value <= 0:
        return
    eng.wait_ge(sem, value)


def wait_apart(eng, sem, value):
    eng.wait_ge(sem, 1)
    eng.wait_ge(sem, value)


def f32(ap):
    return ap.bitcast(F32)


def column(ap):
    return ap.rearrange("(t p) -> p t", p=P)


def across(ap):
    n = ap.shape[0]
    return ap.rearrange("(a n) -> a n", a=1).broadcast_to([P, n])


def product(pe, out, stationary, moving, first, last):
    (sh, sl), (mh, ml) = stationary, moving
    pe.matmul(out, sh, mh, start=first, stop=False)
    pe.matmul(out, sh, ml, start=False, stop=False)
    return pe.matmul(out, sl, mh, start=False, stop=last)


class Units:

    def __init__(self):
        self.before, self.k, self.turn, self.per_turn = 0, 0, 0, 0

    def enter(self, turn, per_turn):
        assert per_turn % 2 == 0
        self.before, self.k, self.turn, self.per_turn = self.before + self.k, 0, turn, per_turn

    def leave(self, turns):
        assert self.k == self.per_turn
        self.before, self.k, self.turn = self.before + turns * self.per_turn, 0, 0

    def take(self):
        n = self.before + self.k
        self.k += 1
        return n % 2, self.turn * self.per_turn + (n + 1)


class Room:

    def __init__(self, nc, stack, tag):
        self.nc, self.stack, self.tag, self.all_sems = nc, stack, tag, []

    def sb(self, name, shape, dtype=F32):
        return self.stack.enter_context(self.nc.sbuf_tensor(f"{self.tag}_{name}", shape, dtype))

    def ps(self, name, shape):
        return self.stack.enter_context(self.nc.psum_tensor(f"{self.tag}_{name}", shape, F32))

    def sem(self, name):
        self.all_sems.append(self.stack.enter_context(self.nc.semaphore(f"{self.tag}_{name}")))
        return self.all_sems[-1]

    def sems(self, name, n):
        return [self.sem(f"{name}{k}") for k in range(n)]

    def block(self):
        self.stack.callback(self.clear)
        return self.stack.enter_context(self.nc.Block())

    def clear(self):
        for sem in self.all_sems:
            self.nc.gpsimd.sem_clear(sem)
        self.nc.all_engine_barrier()


def make_identity(pool, ident, made):
    pool.memset(ident[:, :], 0.0).then_inc(made, 1)
    pool.wait_ge(made, 1)
    pool.affine_select(out=ident[:, :], in_=ident[:, :], compare_op=ALU.not_equal, fill=1.0, base=0,
                       pattern=[[-1, P]], channel_multiplier=1).then_inc(made, 1)


def nonlocal_phase(nc, a, m2t_dram, cb_dram):
    OC = S // P
    with ExitStack() as stack:
        r = Room(nc, stack, "N")
        ident = r.sb("ident", [P, P])
        raw_pg = r.sb("raw_pg", [P, 2, S])
        pg_h = r.sb("pg_h", [P, OC, 2 * CI], F32R)
        pg_l = r.sb("pg_l", [P, OC, 2 * CI], F32R)
        pg_bias = r.sb("pg_bias", [P, 2 * CI])
        theta = r.sb("theta", [P, S])
        theta_b = r.sb("theta_b", [P, 1])
        raw_w = r.sb("raw_w", [P, OC, CI])
        w_s = r.sb("w_s", [P, OC, CI])
        w_t = r.sb("w_t", [P, S])
        bn = r.sb("bn", [P, 5, OC])
        ve = r.sb("ve", [P, OC])
        half = r.sb("half", [P, OC])
        inv = r.sb("inv", [P, OC])
        gain = r.sb("gain", [P, OC])
        fix0 = r.sb("fix0", [P, OC])
        fix1 = r.sb("fix1", [P, OC])
        fix = r.sb("fix", [P, OC])
        ctx = r.sb("ctx", [P, 2, OC, H])
        ctx_h = r.sb("ctx_h", [P, 2, OC, H], F32R)
        ctx_l = r.sb("ctx_l", [P, 2, OC, H], F32R)
        pg = r.sb("pg", [P, 2, KT, 2 * CI])
        pgt = r.sb("pgt", [P, 2, CI])
        m1t = r.sb("m1t", [P, 2, S])
        m2t = r.sb("m2t", [P, 2, OC * S])
        cb = r.sb("cb", [P, 2, OC])
        big = r.ps("big", [P, 4, 512])
        small = r.ps("small", [P, 4, 512])

        ld_c, made, pe_prep, po, fixed = (r.sem(n) for n in ("ld_c", "made", "pe_prep", "po", "fixed"))
        ws_done, wh_done, wl_done, wt_done = (r.sem(n) for n in ("ws_done", "wh_done", "wl_done", "wt_done"))
        ld = r.sems("ld", 2)
        split_h, split_l = r.sem("split_h"), r.sem("split_l")
        ev_pg, ev_1, ev_2, ev_3, ev_b = (r.sem(n) for n in ("ev_pg", "ev_1", "ev_2", "ev_3", "ev_b"))
        mm_pg, mm_1, mm_2, mm_3, mm_b = (r.sem(n) for n in ("mm_pg", "mm_1", "mm_2", "mm_3", "mm_b"))
        st = r.sems("st", 2)
        block = r.block()
        ctx_d = a["ctx"].rearrange("b (t p) n -> b p t n", p=P)
        CONSTS = 12

        def steps(eng, step):
            step(1, 1)
            with eng.Fori(1, B // 2 - 1) as i:
                step(i * 2, 0)
                step(i * 2 + 1, 1)
            step(B - 2, 0)
            step(B - 1, 1)

        @block.sync
        def _(sp):
            def small_load(dst, src):
                sp.dma_start(dst, src, allow_slow_non_contiguous=True).then_inc(ld_c, DMA)
            small_load(raw_pg[:, 0, :], a["phi_w"])
            small_load(raw_pg[:, 1, :], a["g_w"])
            for b in range(2):
                sp.dma_start(ctx[:, b, :, :], ctx_d[b]).then_inc(ld[b], DMA)
            small_load(theta[:, :], a["theta_w"])
            small_load(raw_w[:, :, :], a["w_w"].rearrange("(t p) c -> p t c", p=P))
            for k, n in enumerate(("bn_gamma", "bn_beta", "bn_mean", "bn_var", "w_b")):
                small_load(bn[:, k, :], column(a[n]))
            small_load(pg_bias[:, 0:CI], across(a["phi_b"]))
            small_load(pg_bias[:, CI:], across(a["g_b"]))
            sp.dma_start(theta_b[:, :], column(a["theta_b"]), allow_slow_non_contiguous=True).then_inc(ld_c, DMA)

            def load(b, par):
                wait(sp, split_l, b - 1)
                sp.dma_start(ctx[:, par, :, :], ctx_d[b]).then_inc(ld[par], DMA)

            def store(b, par):
                sp.wait_ge(ev_3, b + 1)
                sp.dma_start(m2t_dram[b], m2t[:, par, :]).then_inc(st[par], DMA)
                sp.wait_ge(ev_b, b + 1)
                sp.dma_start(cb_dram[b], cb[:, par, :]).then_inc(st[par], DMA)
            load(2, 0)
            with sp.Fori(1, B // 2 - 1) as i:
                load(i * 2 + 1, 1)
                store(i * 2 - 2, 0)
                load(i * 2 + 2, 0)
                store(i * 2 - 1, 1)
            load(B - 1, 1)
            for n in range(4):
                store(B - 4 + n, n % 2)
            for par in range(2):
                sp.wait_ge(st[par], 2 * DMA * (B // 2))

        @block.gpsimd
        def _(pool):
            make_identity(pool, ident, made)
            pool.memset(half[:, :], -0.5).then_inc(po, 1)
            pool.wait_ge(ld_c, CONSTS * DMA)
            pool.wait_ge(po, 1)
            pool.tensor_scalar(ve[:, :], bn[:, 3, :], EPS, None, ALU.add).then_inc(po, 1)
            pool.wait_ge(po, 2)
            pool.tensor_tensor(inv[:, :], ve[:, :], half[:, :], ALU.pow).then_inc(po, 1)


        @block.tensor
        def _(pe):
            pe.wait_ge(made, 2)
            pe.wait_ge(ld_c, CONSTS * DMA)
            for w in range(2):
                for t in range(OC):
                    last = pe.transpose(big[:, t, w * CI:(w + 1) * CI], raw_pg[:, w, t * P:(t + 1) * P], ident[:, :])
            last.then_inc(pe_prep, 1)
            pe.wait_ge(ws_done, OC)
            for t in range(OC):
                last = pe.transpose(small[:, 0, t * P:(t + 1) * P], w_s[:, t, :], ident[:, :])
            last.then_inc(pe_prep, 1)
            pe.wait_ge(wl_done, 1)
            pe.wait_ge(wt_done, 1)

            def phi_g(b, par, m):
                if m == 0:
                    pe.wait_ge(split_l, b + 1)
                    wait(pe, ev_pg, 2 * b - 2)
                out = big[:, 2 * par + m // 2, (m % 2) * S:(m % 2 + 1) * S]
                for t in range(OC):
                    cols = slice(m * P, (m + 1) * P)
                    last = product(pe, out, (ctx_h[:, par, t, cols], ctx_l[:, par, t, cols]),
                                   (pg_h[:, t, :], pg_l[:, t, :]), t == 0, t == OC - 1)
                if m % 2:
                    last.then_inc(mm_pg, 1)

            def chain_1(b, par):
                pe.wait_ge(ev_pg, 2 * b + 2)
                for m in range(KT):
                    last = pe.matmul(small[:, 0, 0:CI], pg[:, par, m, CI:], pg[:, par, m, 0:CI],
                                     start=(m == 0), stop=(m == KT - 1))
                last.then_inc(mm_1, 1)

            def chain_2(b, par):
                pe.wait_ge(ev_1, b + 1)
                pe.matmul(small[:, 1, 0:S], pgt[:, par, :], w_t[:, :], start=True, stop=True).then_inc(mm_2, 1)

            def chain_3(b, par):
                pe.wait_ge(ev_2, b + 1)
                wait(pe, ev_3, b)
                for t in range(OC):
                    last = pe.matmul(small[:, 2, t * S:(t + 1) * S], theta[:, t * P:(t + 1) * P], m1t[:, par, :],
                                     start=True, stop=True)
                last.then_inc(mm_3, 1)
                wait(pe, ev_b, b)
                for t in range(OC):
                    last = pe.matmul(small[:, 3, t:t + 1], m1t[:, par, t * P:(t + 1) * P], theta_b[:, :],
                                     start=True, stop=True)
                last.then_inc(mm_b, 1)

            def step(b, par):
                phi_g(b, par, 0)
                phi_g(b, par, 1)
                chain_1(b - 1, 1 - par)
                phi_g(b, par, 2)
                chain_2(b - 1, 1 - par)
                phi_g(b, par, 3)
                chain_3(b - 1, 1 - par)
            for m in range(KT):
                phi_g(0, 0, m)
            steps(pe, step)
            chain_1(B - 1, 1)
            chain_2(B - 1, 1)
            chain_3(B - 1, 1)

        @block.scalar
        def _(act):
            act.wait_ge(pe_prep, 1)
            act.activation(pg_h[:, :, :], big[:, 0:OC, 0:2 * CI], ACT.Copy).then_inc(wh_done, 1)

            def hi(b, par):
                act.wait_ge(ld[par], (b - par) * (DMA // 2) + DMA)
                wait(act, mm_pg, 2 * b - 2)
                act.activation(ctx_h[:, par, :, :], ctx[:, par, :, :], ACT.Copy).then_inc(split_h, 1)

            def out(b, par):
                act.wait_ge(mm_1, b + 1)
                act.activation(pgt[:, par, :], small[:, 0, 0:CI], ACT.Copy).then_inc(ev_1, 1)
                act.wait_ge(mm_2, b + 1)
                act.activation(m1t[:, par, :], small[:, 1, 0:S], ACT.Copy).then_inc(ev_2, 1)
                act.wait_ge(mm_3, b + 1)
                wait(act, st[par], (b - par) * DMA)
                act.activation(m2t[:, par, :], small[:, 2, :], ACT.Copy).then_inc(ev_3, 1)

            def step(b, par):
                if not (isinstance(b, int) and b == B - 1):
                    hi(b + 1, 1 - par)
                out(b - 1, 1 - par)
            hi(0, 0)
            hi(1, 1)
            steps(act, step)
            out(B - 1, 1)

        @block.vector
        def _(dve):
            dve.wait_ge(po, 3)
            n = 0

            def link(ins):
                nonlocal n
                n += 1
                ins.then_inc(fixed, 1)
                dve.wait_ge(fixed, n)
            link(dve.tensor_tensor(gain[:, :], bn[:, 0, :], inv[:, :], ALU.mult))
            link(dve.tensor_tensor(fix0[:, :], bn[:, 4, :], bn[:, 2, :], ALU.subtract))
            link(dve.tensor_tensor(fix1[:, :], fix0[:, :], gain[:, :], ALU.mult))
            link(dve.tensor_tensor(fix[:, :], fix1[:, :], bn[:, 1, :], ALU.add))
            for t in range(OC):
                last = dve.tensor_scalar(w_s[:, t, :], raw_w[:, t, :], gain[:, t:t + 1], 1.0 / H, ALU.mult, ALU.mult)
                last.then_inc(ws_done, 1)
            dve.wait_ge(wh_done, 1)
            dve.tensor_tensor(pg_l[:, :, :], big[:, 0:OC, 0:2 * CI], f32(pg_h[:, :, :]), ALU.subtract).then_inc(wl_done, 1)
            dve.wait_ge(pe_prep, 2)
            dve.tensor_copy(w_t[:, :], small[:, 0, 0:S]).then_inc(wt_done, 1)

            def lo(b, par):
                dve.wait_ge(split_h, b + 1)
                wait(dve, mm_pg, 2 * b - 2)
                dve.tensor_tensor(ctx_l[:, par, :, :], ctx[:, par, :, :], f32(ctx_h[:, par, :, :]), ALU.subtract)\
                   .then_inc(split_l, 1)

            def add_bias(b, par):
                for n in range(2):
                    dve.wait_ge(mm_pg, 2 * b + (n + 1))
                    wait(dve, mm_1, b - 1)
                    dve.tensor_tensor(pg[:, par, 2 * n:2 * n + 2, :],
                                      big[:, 2 * par + n, :].rearrange("p (m c) -> p m c", m=2),
                                      pg_bias[:, :].unsqueeze(1).to_broadcast([P, 2, 2 * CI]), ALU.add).then_inc(ev_pg, 1)

            def bias(b, par):
                dve.wait_ge(mm_b, b + 1)
                wait(dve, st[par], (b - par) * DMA)
                dve.tensor_tensor(cb[:, par, :], small[:, 3, 0:OC], fix[:, :], ALU.add).then_inc(ev_b, 1)

            def step(b, par):
                if not (isinstance(b, int) and b == B - 1):
                    lo(b + 1, 1 - par)
                add_bias(b, par)
                bias(b - 1, 1 - par)
            lo(0, 0)
            lo(1, 1)
            add_bias(0, 0)
            steps(dve, step)
            bias(B - 1, 1)


def attention_phase(nc, tag, rows, context, mask, weights, biases, out_bias, ln_s, ln_b, out):
    cross = context is not None
    with ExitStack() as stack:
        r = Room(nc, stack, tag)
        ident = r.sb("ident", [P, P])
        w_h = r.sb("w_h", [P, KT, 4 * H], F32R)
        w_l = r.sb("w_l", [P, KT, 4 * H], F32R)
        lns = r.sb("lns", [P, KT])
        lns_q = r.sb("lns_q", [P, KT])
        lnb = r.sb("lnb", [P, KT])
        bias_in = r.sb("bias_in", [P, 3, KT])
        bias_sum = r.sb("bias_sum", [P, 3, KT])
        bias_q = r.sb("bias_q", [P, KT])
        o_bias = r.sb("o_bias", [P, H])
        half = r.sb("half", [P, TT])
        eps = r.sb("eps", [P, TT])
        big_one = r.sb("big_one", [P, 2])
        n_mask = BPB if cross else 1
        mk = r.sb("mk", [P, n_mask, TPB, S])
        ma = r.sb("ma", [P, n_mask, TPB, S])
        x = r.sb("x", [P, TT, H])
        stats = r.sb("stats", [P, TT, 6])
        mv = r.sb("mv", [P, TT, 2])
        ve = r.sb("ve", [P, TT])
        rstd = r.sb("rstd", [P, TT])
        xt_h = r.sb("xt_h", [P, KT, TOK], F32R)
        xt_l = r.sb("xt_l", [P, KT, TOK], F32R)
        if cross:
            e = r.sb("e", [P, 2, H])
            et_h = r.sb("et_h", [P, KT, TOK], F32R)
            et_l = r.sb("et_l", [P, KT, TOK], F32R)
        else:
            et_h, et_l = xt_h, xt_l
        q_h = r.sb("q_h", [P, KT, TOK], F32R)
        q_l = r.sb("q_l", [P, KT, TOK], F32R)
        k_h = r.sb("k_h", [P, KT, TOK], F32R)
        k_l = r.sb("k_l", [P, KT, TOK], F32R)
        v = r.sb("v", [P, TT, H])
        p = r.sb("p", [P, 2, HPG, TPB, S])
        raw = p[:, 1, :, :, :].rearrange("p j t s -> p j (t s)")
        nmax = r.sb("nmax", [P, 2, HPG, TPB])
        rsum = r.sb("rsum", [P, 2, HPG, TPB])
        rinv = r.sb("rinv", [P, 2, HPG, TPB])
        rwide = r.sb("rwide", [P, 2, TPB, P])
        pt = r.sb("pt", [P, HPG, TPB, S])
        rt = r.sb("rt", [P, S])
        cx = r.sb("cx", [P, S])
        ct_h = r.sb("ct_h", [P, KT, TOK], F32R)
        ct_l = r.sb("ct_l", [P, KT, TOK], F32R)
        res = r.sb("res", [P, 2, H])
        sc = r.ps("sc", [P, HPG, 512])
        tp = r.ps("tp", [P, 2, 512])
        banks = r.ps("banks", [P, 2, 512])

        made, half_ok, ld_c = r.sem("made"), r.sem("half_ok"), r.sem("ld_c")
        ld_w = r.sems("ld_w", KT)
        ld_x, ld_e = r.sems("ld_x", TT), (r.sems("ld_e", 2) if cross else None)
        ld_r, st_y, ld_m = r.sems("ld_r", 2), r.sems("st_y", 2), r.sems("ld_m", n_mask)
        w_hi, w_lo = r.sem("w_hi"), r.sem("w_lo")
        folded, bias_ok, bias_q_ok, lns_ok = (r.sem(n) for n in ("folded", "bias_ok", "bias_q_ok", "lns_ok"))
        ln_st, ln_mv, ln_ve, ln_rs, ln_x = (r.sem(n) for n in ("ln_st", "ln_mv", "ln_ve", "ln_rs", "ln_x"))
        done = r.sem("done")
        x_hi, x_lo, e_hi, e_lo = (r.sem(n) for n in ("x_hi", "x_lo", "e_hi", "e_lo"))
        q_hi, q_lo, k_hi, k_lo, v_ok = (r.sem(n) for n in ("q_hi", "q_lo", "k_hi", "k_lo", "v_ok"))
        scored, masked, biased, exped = (r.sem(n) for n in ("scored", "masked", "biased", "exped"))
        inv_ok, wide_ok = r.sem("inv_ok"), r.sem("wide_ok")
        turned, pt_ok = r.sem("turned"), r.sem("pt_ok")
        rt_ok, cx_ok, c_hi, c_lo = (r.sem(n) for n in ("rt_ok", "cx_ok", "c_hi", "c_lo"))
        res_ok, y_ok, m_ok, m1_ok = (r.sem(n) for n in ("res_ok", "y_ok", "m_ok", "m1_ok"))
        block = r.block()

        scale = float(HD) ** -0.5
        xd = rows.rearrange("b (t p) n -> (b t) p n", p=P)
        ed = context.rearrange("b (t p) n -> (b t) p n", p=P) if cross else None
        yd = out.rearrange("b (t p) n -> (b t) p n", p=P)
        md = mask.rearrange("b a (t p) n -> (b a) p t n", p=P)
        fold = [True, not cross, not cross]
        n_consts = 2 + 3 + 1
        src_lo = e_lo if cross else x_lo

        def factor(c, t):
            if c == 0:
                return lns_q[:, t:t + 1]
            return lns[:, t:t + 1] if c < 3 and fold[c] else 1.0

        def in_slot(g, first, last):
            xs = [(c, t, 1) for t in (2 * g - 4, 2 * g - 3) for c in ("x", "e") if c == "x" or cross]
            pre, post = [
                ([("o", 1, -1)], [("v", 2, 0)]),
                ([("v", 3, 0)], [("o", 2, -1)]),
                (xs, [("o", 3, -1)]),
                (xs, []),
                ([("q", 0, 1)], [("k", 0, 1), ("v", 0, 1)]),
                ([("q", 1, 1)], [("k", 1, 1), ("v", 1, 1)]),
                ([("q", 2, 1)], [("k", 2, 1)]),
                ([("q", 3, 1)], [("k", 3, 1), ("o", 0, 0)]),
            ][g]
            runs = lambda u: not (first and u[2] < 0) and not (last and u[2] > 0)
            return list(filter(runs, pre)), list(filter(runs, post))
        PER_BLOCK = NG + sum(len(a_) + len(b_) for a_, b_ in (in_slot(g, False, False) for g in range(NG)))
        BEFORE = [(c, t, 1) for t in range(TT) for c in ("x", "e") if c == "x" or cross] + \
            [(c, n, 1) for n in range(KT) for c in ("q", "k")] + [("v", 0, 1), ("v", 1, 1)]
        AFTER = [("o", n, -1) for n in (1, 2, 3)]

        def read_out(unit, blk):
            kind, n, rel = unit
            if kind == "pv":
                return cx_ok, (blk + rel) * NG + n
            sem, per = {"x": (x_lo, TT), "e": (e_lo, TT), "q": (q_lo, KT), "k": (k_lo, KT), "v": (v_ok, TT),
                        "o": (y_ok, TT)}[kind]
            return sem, (blk + rel) * per + (n + 1)

        def phase(eng, before, slot, after):
            units = Units()
            before([(u, units.take()) for u in BEFORE])

            def body(blk, first, last):
                for g in range(NG):
                    pre, post = in_slot(g, first, last)
                    pre = [(u, units.take()) for u in pre]
                    pv = None if first and g == 0 else units.take()
                    slot(blk, g, first, last, pre, pv, [(u, units.take()) for u in post])
            body(0, True, False)
            with eng.Fori(1, NB - 1) as i:
                units.enter(i - 1, PER_BLOCK)
                body(i, False, False)
            units.leave(NB - 2)
            body(NB - 1, False, True)
            after(units.take(), [(u, units.take()) for u in AFTER])

        @block.sync
        def _(sp):
            def const(dst, src):
                sp.dma_start(dst, src, allow_slow_non_contiguous=True).then_inc(ld_c, DMA)

            def load_weights(c):
                for t in range(KT):
                    if c:
                        sp.wait_ge(w_lo, (c - 1) * KT + t + 1)
                        if fold[c - 1]:
                            sp.wait_ge(folded, c)
                    sp.dma_start(raw[:, t, :], weights[c][t * P:(t + 1) * P, :]).then_inc(ld_w[t], DMA)

            def load_rows(blk, first):
                for t in range(TT):
                    if not first:
                        sp.wait_ge(x_lo, (blk - 1) * TT + (t + 1))
                    sp.dma_start(x[:, t, :], xd[blk * TT + t]).then_inc(ld_x[t], DMA)
                    if cross and first and t < 2:
                        load_context(blk, t)

            def load_context(blk, t):
                wait(sp, e_lo, blk * TT + (t - 1))
                sp.dma_start(e[:, t % 2, :], ed[blk * TT + t]).then_inc(ld_e[t % 2], DMA)

            def load_res(blk, t):
                wait(sp, st_y[t % 2], (blk * 2 + t // 2) * DMA)
                sp.dma_start(res[:, t % 2, :], xd[blk * TT + t]).then_inc(ld_r[t % 2], DMA)

            def store(blk, t):
                sp.wait_ge(y_ok, blk * TT + (t + 1))
                sp.dma_start(yd[blk * TT + t], res[:, t % 2, :]).then_inc(st_y[t % 2], DMA)

            load_rows(0, True)
            const(lns[:, :], column(ln_s))
            const(lnb[:, :], column(ln_b))
            load_weights(0)
            for c in range(3):
                const(bias_in[:, c, :], column(biases[c]))
            const(o_bias[:, :], across(out_bias))
            for b in range(n_mask):
                sp.dma_start(mk[:, b, :, :], md[b]).then_inc(ld_m[b], DMA)
            if cross:
                load_context(0, 2)
                load_context(0, 3)
            for c in range(1, 4):
                load_weights(c)
            load_res(0, 0)
            load_res(0, 1)

            def body(blk, first, last):
                if not last:
                    load_rows(blk + 1, False)
                    if cross:
                        load_context(blk + 1, 0)
                        load_context(blk + 1, 1)
                if not first:
                    store(blk - 1, 1)
                    load_res(blk - 1, 3)
                    store(blk - 1, 2)
                    load_res(blk, 0)
                if cross and not last:
                    load_context(blk + 1, 2)
                    load_context(blk + 1, 3)
                if not first:
                    store(blk - 1, 3)
                    load_res(blk, 1)
                if cross and not last:
                    for b in range(BPB):
                        sp.wait_ge(biased, (blk * NG + (b + 1) * KT) * HPG * TPB)
                        sp.dma_start(mk[:, b, :, :], md[(blk + 1) * BPB + b]).then_inc(ld_m[b], DMA)
                store(blk, 0)
                load_res(blk, 2)
            body(0, True, False)
            with sp.Fori(1, NB - 1) as i:
                body(i, False, False)
            body(NB - 1, False, True)
            store(NB - 1, 1)
            load_res(NB - 1, 3)
            store(NB - 1, 2)
            store(NB - 1, 3)
            for n in range(2):
                sp.wait_ge(st_y[n], DMA * (B * TPB // 2))

        @block.gpsimd
        def _(pool):
            def normalise(blk):
                pool.wait_ge(ln_mv, blk + 1)
                pool.tensor_tensor(ve[:, :], mv[:, :, 1], eps[:, :], ALU.add).then_inc(ln_ve, 1)
                pool.wait_ge(ln_ve, blk + 1)
                pool.tensor_tensor(rstd[:, :], ve[:, :], half[:, :], ALU.pow).then_inc(ln_rs, 1)
                wait_apart(pool, ln_rs, blk + 1)
                for t in range(TT):
                    pool.tensor_scalar(x[:, t, :], x[:, t, :], mv[:, t, 0:1], rstd[:, t:t + 1],
                                       ALU.subtract, ALU.mult).then_inc(ln_x, 1)

            def add_bias(blk, t):
                pool.wait_ge(ld_r[t % 2], (blk * 2 + (t // 2 + 1)) * DMA)
                pool.tensor_tensor(res[:, t % 2, :], res[:, t % 2, :], o_bias[:, :], ALU.add).then_inc(res_ok, 1)

            def addend(blk, b):
                n = blk * n_mask + (b + 1)
                whole = lambda c: big_one[:, c:c + 1].unsqueeze(2).to_broadcast([P, TPB, S])
                pool.wait_ge(ld_m[b], (blk + 1) * DMA)
                pool.tensor_tensor(ma[:, b, :, :], mk[:, b, :, :], whole(0), ALU.subtract).then_inc(m1_ok, 1)
                pool.wait_ge(m1_ok, n)
                pool.tensor_tensor(ma[:, b, :, :], ma[:, b, :, :], whole(1), ALU.mult).then_inc(m_ok, 1)

            make_identity(pool, ident, made)
            for tile, value in ((half[:, :], -0.5), (eps[:, :], EPS), (big_one[:, 0:1], 1.0), (big_one[:, 1:2], 10000.0)):
                pool.memset(tile, value).then_inc(half_ok, 1)
            pool.wait_ge(half_ok, 4)
            normalise(0)
            for b in range(n_mask):
                addend(0, b)
            pool.wait_ge(ld_c, n_consts * DMA)
            add_bias(0, 0)
            add_bias(0, 1)

            def body(blk, first, last):
                if not last:
                    normalise(blk + 1)
                if not first:
                    add_bias(blk - 1, 3)
                    add_bias(blk, 0)
                    add_bias(blk, 1)
                if cross and not last:
                    for b in range(BPB):
                        addend(blk + 1, b)
                add_bias(blk, 2)
            body(0, True, False)
            with pool.Fori(1, NB - 1) as i:
                body(i, False, False)
            body(NB - 1, False, True)
            add_bias(NB - 1, 3)

        @block.tensor
        def _(pe):
            in_bank = [None, None]

            def occupy(unit, bank, blk):
                if in_bank[bank] is not None:
                    wait(pe, *read_out(in_bank[bank], blk))
                in_bank[bank] = unit

            def fold_bias(c):
                for t in range(KT):
                    pe.wait_ge(ld_w[t], (c + 1) * DMA)
                for f in range(KT):
                    for t in range(KT):
                        last = pe.matmul(sc[:, c, f:f + 1], raw[:, t, f * P:(f + 1) * P],
                                         lnb[:, t:t + 1], start=(t == 0), stop=(t == KT - 1))
                last.then_inc(folded, 1)

            def steps_of(item, blk, first):
                unit, (bank, _) = item
                kind, n, rel = unit
                tb = blk + rel
                o = banks[:, bank, :]

                def transposes():
                    occupy(unit, bank, blk)
                    if kind == "x":
                        pe.wait_ge(ln_x, tb * TT + (n + 1))
                    else:
                        pe.wait_ge(ld_e[n % 2], (tb * 2 + (n // 2 + 1)) * DMA)
                    src = x[:, n, :] if kind == "x" else e[:, n % 2, :]
                    for f in range(KT):
                        last = pe.transpose(o[:, f * P:(f + 1) * P], src[:, f * P:(f + 1) * P], ident[:, :])
                    last.then_inc(done, 1)
                if kind in "xe":
                    return [transposes]
                cols = slice(n * P, (n + 1) * P)
                part = "qkvo".index(kind)
                wcols = slice(part * H, (part + 1) * H) if kind in "vo" else slice(part * H + n * P, part * H + (n + 1) * P)
                sh, sl = {"q": (xt_h, xt_l), "k": (et_h, et_l), "v": (et_h, et_l), "o": (ct_h, ct_l)}[kind]

                def step(t):
                    if t == 0:
                        occupy(unit, bank, blk)
                        if first:
                            pe.wait_ge(w_lo, (part + 1) * KT)
                        if kind == "q":
                            pe.wait_ge(x_lo, (tb + 1) * TT)
                        elif kind == "k":
                            pe.wait_ge(src_lo, (tb + 1) * TT)
                        elif kind == "v":
                            pe.wait_ge(src_lo, tb * TT + (n + 1))
                        else:
                            pe.wait_ge(c_lo, tb * NG + (n // TPB + 1) * KT)
                    w = (w_h[:, t, wcols], w_l[:, t, wcols])
                    if kind in "qk":
                        last = product(pe, o, w, (sh[:, t, :], sl[:, t, :]), t == 0, t == KT - 1)
                    else:
                        last = product(pe, o, (sh[:, t, cols], sl[:, t, cols]), w, t == 0, t == KT - 1)
                    if t == KT - 1:
                        last.then_inc(done, 1)
                return [lambda t=t: step(t) for t in range(KT)]

            def run(items, blk, first):
                for item in items:
                    for s in steps_of(item, blk, first):
                        s()

            def scores(blk, g):
                b, f = g // KT, g % KT
                grp = blk * NG + g
                pe.wait_ge(q_lo, blk * KT + (f + 1))
                pe.wait_ge(k_lo, blk * KT + (f + 1))
                wait(pe, masked, grp)
                for t in range(TPB):
                    rows_, keys = slice(b * S + t * P, b * S + (t + 1) * P), slice(b * S, (b + 1) * S)
                    for n, (qp, kp) in enumerate(((q_h, k_h), (q_h, k_l), (q_l, k_h))):
                        for j in range(HPG):
                            rr = slice(j * HD, (j + 1) * HD)
                            last = pe.matmul(sc[:, j, t * S:(t + 1) * S], qp[rr, f, rows_], kp[rr, f, keys],
                                             start=(n == 0), stop=(n == 2))
                last.then_inc(scored, 1)

            def turn(blk, g, j):
                grp = blk * NG + g
                pe.wait_ge(exped, grp * HPG * TPB + (j + 1) * TPB)
                wait(pe, pt_ok, grp * HPG + (j - 1))
                for t in range(TPB):
                    for c in range(TPB):
                        last = pe.transpose(tp[:, j % 2, c * S + t * P:c * S + (t + 1) * P],
                                            p[:, g % 2, j, t, c * P:(c + 1) * P], ident[:, :])
                last.then_inc(turned, 1)

            def weigh(blk, g, bank, now, rel):
                b, f = g // KT, g % KT
                grp = blk * NG + g
                occupy(("pv", g + 1, rel), bank, now)
                pe.wait_ge(wide_ok, grp + 1)
                for t in range(TPB):
                    pe.transpose(banks[:, bank, S + t * P:S + (t + 1) * P], rwide[:, g % 2, t, :], ident[:, :])
                pe.wait_ge(pt_ok, (grp + 1) * HPG)
                pe.wait_ge(v_ok, blk * TT + (b + 1) * TPB)
                for c in range(TPB):
                    for j in range(HPG):
                        rr = slice(j * HD, (j + 1) * HD)
                        last = pe.matmul(banks[rr, bank, 0:S], v[:, b * TPB + c, f * P + j * HD:f * P + (j + 1) * HD],
                                         pt[:, j, c, :], start=(c == 0), stop=(c == TPB - 1))
                last.then_inc(done, 1)

            def before(items):
                pe.wait_ge(made, 2)
                pe.wait_ge(ld_c, n_consts * DMA)
                fold_bias(0)
                n = TT * (2 if cross else 1)
                run(items[:n], -1, True)
                for c in (1, 2):
                    if fold[c]:
                        fold_bias(c)
                run(items[n:n + 2], -1, True)
                pe.wait_ge(bias_ok, 3)
                scores(0, 0)
                run(items[n + 2:], -1, True)
                for b in range(2):
                    kind, m, rel = in_bank[b]
                    in_bank[b] = kind, m, rel - 1

            def slot(blk, g, first, last, pre, pv, post):
                if g == 0 and not first:
                    for b in range(2):
                        kind, n, rel = in_bank[b]
                        in_bank[b] = kind, n, rel - 1
                pb, pg, rel = (blk, g - 1, 0) if g else (blk - 1, NG - 1, -1)
                steps = [s for item in pre for s in steps_of(item, blk, first)]
                for j in range(HPG):
                    if pv is not None:
                        turn(pb, pg, j)
                    for s in steps[j * len(steps) // HPG:(j + 1) * len(steps) // HPG]:
                        s()
                if g + 1 < NG:
                    scores(blk, g + 1)
                elif not last:
                    scores(blk + 1, 0)
                if pv is not None:
                    weigh(pb, pg, pv[0], blk, rel)
                run(post, blk, first)

            def after(pv, items):
                for b in range(2):
                    kind, n, rel = in_bank[b]
                    in_bank[b] = kind, n, rel - 1
                for j in range(HPG):
                    turn(NB - 1, NG - 1, j)
                weigh(NB - 1, NG - 1, pv[0], NB, -1)
                run(items, NB, False)
            phase(pe, before, slot, after)

        @block.scalar
        def _(act):
            def split_weights(c):
                for t in range(KT):
                    act.wait_ge(ld_w[t], (c + 1) * DMA)
                    act.activation(w_h[:, t, c * H:(c + 1) * H], raw[:, t, :], ACT.Copy,
                                   scale=factor(c, t)).then_inc(w_hi, 1)

            def read(item, blk, first):
                (kind, n, rel), (bank, count) = item
                o = banks[:, bank, :]
                if kind == "o":
                    return
                act.wait_ge(done, count)
                if kind in "xe":
                    dst, sem = (xt_h, x_hi) if kind == "x" else (et_h, e_hi)
                    act.activation(dst[:, :, n * P:(n + 1) * P], o.rearrange("p (f c) -> p f c", f=KT), ACT.Copy)\
                       .then_inc(sem, 1)
                elif kind in "qk":
                    if first:
                        act.wait_ge(bias_q_ok, 1)
                        act.wait_ge(bias_ok, 2)
                    dst, bias, sem = (q_h, bias_q, q_hi) if kind == "q" else (k_h, bias_sum[:, 1, :], k_hi)
                    act.activation(dst[:, n, :], o, ACT.Identity, bias=bias[:, n:n + 1]).then_inc(sem, 1)
                else:
                    act.activation(v[:, n, :], o, ACT.Copy).then_inc(v_ok, 1)

            def exponentials(blk, g, j):
                grp = blk * NG + g
                for t in range(TPB):
                    act.wait_ge(biased, grp * HPG * TPB + (j * TPB + t + 1))
                    act.activation(p[:, g % 2, j, t, :], p[:, g % 2, j, t, :], ACT.Exp, scale=-1.0,
                                   bias=nmax[:, g % 2, j, t:t + 1], accum_out=rsum[:, g % 2, j, t:t + 1])\
                       .then_inc(exped, 1)

            def turned_out(blk, g, j):
                grp = blk * NG + g
                act.wait_ge(turned, grp * HPG + (j + 1))
                act.activation(pt[:, j, :, :], tp[:, j % 2, :].rearrange("p (c s) -> p c s", c=TPB), ACT.Copy)\
                   .then_inc(pt_ok, 1)

            def weighed(blk, g, pv):
                b, f = g // KT, g % KT
                grp = blk * NG + g
                bank, count = pv
                act.wait_ge(done, count)
                wait(act, cx_ok, grp)
                act.activation(rt[:, :], banks[:, bank, S:2 * S], ACT.Copy).then_inc(rt_ok, 1)
                act.wait_ge(cx_ok, grp + 1)
                act.activation(ct_h[:, f, b * S:(b + 1) * S], cx[:, :], ACT.Identity, bias=bias_sum[:, 2, f:f + 1])\
                   .then_inc(c_hi, 1)

            def before(items):
                n = TT * (2 if cross else 1)
                act.wait_ge(lns_ok, 1)
                split_weights(0)
                for item in items[:n]:
                    read(item, -1, True)
                split_weights(1)
                split_weights(2)
                read(items[n], -1, True)
                read(items[n + 1], -1, True)
                split_weights(3)
                for item in items[n + 2:]:
                    read(item, -1, False)
                act.wait_ge(bias_ok, 3)

            def slot(blk, g, first, last, pre, pv, post):
                pb, pg = (blk, g - 1) if g else (blk - 1, NG - 1)
                for j in range(HPG):
                    if pv is not None:
                        turned_out(pb, pg, j)
                    exponentials(blk, g, j)
                    for item in pre[j * len(pre) // HPG:(j + 1) * len(pre) // HPG]:
                        read(item, blk, False)
                if pv is not None:
                    weighed(pb, pg, pv)
                for item in post:
                    read(item, blk, False)

            def after(pv, items):
                for j in range(HPG):
                    turned_out(NB - 1, NG - 1, j)
                weighed(NB - 1, NG - 1, pv)
            phase(act, before, slot, after)

        @block.vector
        def _(dve):
            def split_weights(c):
                for t in range(KT):
                    dve.wait_ge(w_hi, c * KT + t + 1)
                    hi, lo = f32(w_h[:, t, c * H:(c + 1) * H]), w_l[:, t, c * H:(c + 1) * H]
                    if c < 3 and fold[c]:
                        dve.scalar_tensor_tensor(lo, raw[:, t, :], factor(c, t), hi, ALU.mult, ALU.subtract)\
                           .then_inc(w_lo, 1)
                    else:
                        dve.tensor_tensor(lo, raw[:, t, :], hi, ALU.subtract).then_inc(w_lo, 1)

            def biases_of(c):
                if fold[c]:
                    dve.wait_ge(folded, c + 1)
                    dve.tensor_tensor(bias_sum[:, c, :], sc[:, c, 0:KT], bias_in[:, c, :], ALU.add)\
                       .then_inc(bias_ok, 1)
                else:
                    dve.tensor_copy(bias_sum[:, c, :], bias_in[:, c, :]).then_inc(bias_ok, 1)
                if c == 0:
                    dve.wait_ge(bias_ok, 1)
                    dve.tensor_scalar(bias_q[:, :], bias_sum[:, 0, :], scale, None, ALU.mult).then_inc(bias_q_ok, 1)

            def statistics(blk):
                for t in range(TT):
                    dve.wait_ge(ld_x[t], (blk + 1) * DMA)
                    last = dve.bn_stats(stats[:, t, :], x[:, t, :])
                last.then_inc(ln_st, 1)
                wait_apart(dve, ln_st, blk + 1)
                for t in range(TT):
                    last = dve.bn_aggr(mv[:, t, :], stats[:, t, :])
                last.then_inc(ln_mv, 1)

            def read(item, blk):
                (kind, n, rel), (bank, count) = item
                o = banks[:, bank, :]
                tb = blk + rel
                if kind == "v":
                    return
                dve.wait_ge(done, count)
                if kind in "xe":
                    hi, lo, hi_ok, lo_ok = (xt_h, xt_l, x_hi, x_lo) if kind == "x" else (et_h, et_l, e_hi, e_lo)
                    rows_ = slice(n * P, (n + 1) * P)
                    dve.wait_ge(hi_ok, tb * TT + (n + 1))
                    dve.tensor_tensor(lo[:, :, rows_], o.rearrange("p (f c) -> p f c", f=KT), f32(hi[:, :, rows_]),
                                      ALU.subtract).then_inc(lo_ok, 1)
                elif kind in "qk":
                    hi, lo, bias, hi_ok, lo_ok = (q_h, q_l, bias_q, q_hi, q_lo) if kind == "q" else \
                        (k_h, k_l, bias_sum[:, 1, :], k_hi, k_lo)
                    dve.wait_ge(hi_ok, tb * KT + (n + 1))
                    dve.scalar_tensor_tensor(lo[:, n, :], o, bias[:, n:n + 1], f32(hi[:, n, :]), ALU.add, ALU.subtract)\
                       .then_inc(lo_ok, 1)
                else:
                    dve.wait_ge(res_ok, tb * TT + (n + 1))
                    dve.tensor_tensor(res[:, n % 2, :], o, res[:, n % 2, :], ALU.add).then_inc(y_ok, 1)

            def mask_scores(blk, g, first):
                b = g // KT
                grp = blk * NG + g
                if cross:
                    dve.wait_ge(m_ok, blk * BPB + (b + 1))
                elif first:
                    dve.wait_ge(m_ok, 1)
                dve.wait_ge(scored, grp + 1)
                m = mk[:, b % n_mask, :, :].rearrange("p t s -> p (t s)").unsqueeze(1).to_broadcast([P, HPG, TPB * S])
                dve.tensor_tensor(p[:, g % 2, :, :, :].rearrange("p j t s -> p j (t s)"), sc[:, :, :], m, ALU.mult)\
                   .then_inc(masked, 1)
                dve.wait_ge(masked, grp + 1)

            def maxima(blk, g, j):
                b = g // KT
                for t in range(TPB):
                    a_ = p[:, g % 2, j, t, :]
                    dve.tensor_tensor_reduce(out=a_, in0=a_, in1=ma[:, b % n_mask, t, :], scale=-1.0, scalar=BIG,
                                             op0=ALU.add, op1=ALU.min, accum_out=nmax[:, g % 2, j, t:t + 1])\
                       .then_inc(biased, 1)

            def inverses(blk, g):
                grp = blk * NG + g
                dve.wait_ge(exped, (grp + 1) * HPG * TPB)
                dve.reciprocal(rinv[:, g % 2, :, :], rsum[:, g % 2, :, :]).then_inc(inv_ok, 1)
                dve.wait_ge(inv_ok, grp + 1)
                for t in range(TPB):
                    last = dve.tensor_copy(rwide[:, g % 2, t, :].rearrange("p (j d) -> p j d", j=HPG),
                                           rinv[:, g % 2, :, t:t + 1].to_broadcast([P, HPG, HD]))
                last.then_inc(wide_ok, 1)

            def weighed(blk, g, pv):
                b, f = g // KT, g % KT
                grp = blk * NG + g
                bank, count = pv
                dve.wait_ge(rt_ok, grp + 1)
                wait(dve, c_hi, grp)
                dve.tensor_tensor(cx[:, :], banks[:, bank, 0:S], rt[:, :], ALU.mult).then_inc(cx_ok, 1)
                dve.wait_ge(c_hi, grp + 1)
                cols = slice(b * S, (b + 1) * S)
                dve.scalar_tensor_tensor(ct_l[:, f, cols], cx[:, :], bias_sum[:, 2, f:f + 1], f32(ct_h[:, f, cols]),
                                         ALU.add, ALU.subtract).then_inc(c_lo, 1)

            def before(items):
                n = TT * (2 if cross else 1)
                statistics(0)
                dve.wait_ge(ld_c, n_consts * DMA)
                dve.tensor_scalar(lns_q[:, :], lns[:, :], scale, None, ALU.mult).then_inc(lns_ok, 1)
                dve.wait_ge(lns_ok, 1)
                split_weights(0)
                biases_of(0)
                for item in items[:n]:
                    read(item, -1)
                split_weights(1)
                biases_of(1)
                split_weights(2)
                biases_of(2)
                dve.wait_ge(bias_ok, 3)
                read(items[n], -1)
                read(items[n + 1], -1)
                mask_scores(0, 0, True)
                split_weights(3)
                for item in items[n + 2:n + 4]:
                    read(item, -1)
                for j in range(HPG):
                    maxima(0, 0, j)
                for item in items[n + 4:]:
                    read(item, -1)

            def slot(blk, g, first, last, pre, pv, post):
                pb, pg = (blk, g - 1) if g else (blk - 1, NG - 1)
                if g == 1 and not last:
                    statistics(blk + 1)
                for item in pre:
                    read(item, blk)
                nb, ng = (blk, g + 1) if g + 1 < NG else (blk + 1, 0)
                more = g + 1 < NG or not last
                if more:
                    mask_scores(nb, ng, False)
                if pv is not None:
                    weighed(pb, pg, pv)
                inverses(blk, g)
                for j in range(HPG):
                    if more:
                        maxima(nb, ng, j)
                    for item in post[j * len(post) // HPG:(j + 1) * len(post) // HPG]:
                        read(item, blk)

            def after(pv, items):
                weighed(NB - 1, NG - 1, pv)
                for item in items:
                    read(item, NB)
            phase(dve, before, slot, after)


def mlp_phase(nc, rows, w1, b1, w2, b2, ln_s, ln_b, m2t_dram, cb_dram, out):
    with ExitStack() as stack:
        r = Room(nc, stack, "M")
        ident = r.sb("ident", [P, P])
        w1_h = r.sb("w1_h", [P, KT, FF], F32R)
        w1_l = r.sb("w1_l", [P, KT, FF], F32R)
        w2_h = r.sb("w2_h", [P, FT, H], F32R)
        w2_l = r.sb("w2_l", [P, FT, H], F32R)
        ln_scale = r.sb("ln_scale", [P, H])
        ln_shift = r.sb("ln_shift", [P, H])
        b1_col = r.sb("b1_col", [P, FT])
        b2_row = r.sb("b2_row", [P, H])
        half = r.sb("half", [P, TT])
        eps = r.sb("eps", [P, TT])
        x = r.sb("x", [P, TT, H])
        stats = r.sb("stats", [P, TT, 6])
        mv = r.sb("mv", [P, TT, 2])
        ve = r.sb("ve", [P, TT])
        rstd = r.sb("rstd", [P, TT])
        xt_h = r.sb("xt_h", [P, KT, TOK], F32R)
        xt_l = r.sb("xt_l", [P, KT, TOK], F32R)
        hf = r.sb("hf", [P, 2, TOK])
        h_h = r.sb("h_h", [P, 2, TOK], F32R)
        h_l = r.sb("h_l", [P, 2, TOK], F32R)
        t_sb = r.sb("t_sb", [P, TT, H])
        t_h = r.sb("t_h", [P, TPB, H], F32R)
        t_l = r.sb("t_l", [P, TPB, H], F32R)
        m2 = r.sb("m2", [P, TPB * S])
        m2_h = r.sb("m2_h", [P, TPB * S], F32R)
        m2_l = r.sb("m2_l", [P, TPB * S], F32R)
        cb = r.sb("cb", [P, BPB, TPB])
        y = r.sb("y", [P, 2, H])
        acc = r.ps("acc", [P, TT, 512])
        hb = r.ps("hb", [P, 2, 512])
        banks = r.ps("banks", [P, 2, 512])

        made, half_ok, ld_c = r.sem("made"), r.sem("half_ok"), r.sem("ld_c")
        ld_w, ld_x, ld_t, ld_m = r.sems("ld_w", 4), r.sems("ld_x", TT), r.sems("ld_t", TT), r.sem("ld_m")
        ld_b = r.sems("ld_b", BPB)
        st_y = r.sems("st_y", 2)
        w_hi, w_lo = r.sem("w_hi"), r.sem("w_lo")
        ln_st, ln_mv, ln_ve, ln_rs, ln_n, ln_g, ln_x = (r.sem(f"ln_{n}") for n in ("st", "mv", "ve", "rs", "n", "g", "x"))
        done, x_hi, x_lo = r.sem("done"), r.sem("x_hi"), r.sem("x_lo")
        h_done, h_act, h_hi, h_lo = (r.sem(n) for n in ("h_done", "h_act", "h_hi", "h_lo"))
        a_done, t_bias, t_ok = r.sem("a_done"), r.sem("t_bias"), r.sem("t_ok")
        t_hi, t_lo, m2_hi, m2_lo, y_ok = (r.sem(n) for n in ("t_hi", "t_lo", "m2_hi", "m2_lo", "y_ok"))
        block = r.block()

        xd = rows.rearrange("b (t p) n -> (b t) p n", p=P)
        yd = out.rearrange("b (t p) n -> (b t) p n", p=P)
        n_consts = 4

        first_chunks = [(1, t, 0) for t in range(KT)]
        slot_chunks = [[(2, f, 0)] + ([(1, f % KT, f // KT + 1)] if f // KT + 1 < KT else []) for f in range(FT)]
        chunks = first_chunks + [c for s in slot_chunks for c in s]
        number = {c: n for n, c in enumerate(chunks)}

        def parts_of(c):
            m, t, quarter = c
            cols = slice(quarter * 512, (quarter + 1) * 512)
            return (w1_h[:, t, cols], w1_l[:, t, cols]) if m == 1 else (w2_h[:, t, :], w2_l[:, t, :])

        AT = {3: (0, 0), 4: (0, 1), 9: (1, 0), 10: (1, 1)}
        TURNS = [("x", t, 1) for t in range(TT)]

        def read_out(unit, blk):
            kind, n, rel = unit
            if kind == "x":
                return x_lo, (blk + rel) * TT + (n + 1)
            return y_ok, (blk + rel + 1) * TT + (n[0] * TPB + n[1] + 1)

        def phase(eng, before, slot, after):
            units = Units()
            before([(u, units.take()) for u in TURNS])

            def body(blk, first, last):
                for f in range(FT):
                    unit = (("p", AT[f], -1), units.take()) if f in AT and not first else None
                    turns = [(u, units.take()) for u in TURNS] if f == FT - 1 and not last else []
                    slot(blk, f, first, last, unit, turns)
            body(0, True, False)
            with eng.Fori(1, NB - 1) as i:
                units.enter(i - 1, len(AT) + TT)
                body(i, False, False)
            units.leave(NB - 2)
            body(NB - 1, False, True)
            after([(("p", AT[f], -1), units.take()) for f in sorted(AT)])

        @block.sync
        def _(sp):
            def load_chunk(n):
                m, t, quarter = chunks[n]
                if n >= 4:
                    sp.wait_ge(w_lo, n - 3)
                src = w1[t * P:(t + 1) * P, quarter * 512:(quarter + 1) * 512] if m == 1 else w2[t * P:(t + 1) * P, :]
                sp.dma_start(t_sb[:, n % 4, :], src).then_inc(ld_w[n % 4], DMA)

            def load_rows(blk, first):
                for t in range(TT):
                    if not first:
                        sp.wait_ge(x_lo, (blk - 1) * TT + (t + 1))
                    sp.dma_start(x[:, t, :], xd[blk * TT + t]).then_inc(ld_x[t], DMA)

            def load_t(blk, t):
                sp.dma_start(t_sb[:, t, :], xd[blk * TT + t]).then_inc(ld_t[t], DMA)

            def load_m2(blk, b):
                sp.wait_ge(m2_lo, blk * BPB + (b + 1))
                sp.dma_start(m2[:, :], m2t_dram[blk * BPB + b]).then_inc(ld_m, DMA)
                sp.wait_ge(y_ok, blk * TT + (b + 1) * TPB)
                sp.dma_start(cb[:, b, :], cb_dram[blk * BPB + b]).then_inc(ld_b[b], DMA)

            def store(blk, b, t):
                sp.wait_ge(y_ok, (blk + 1) * TT + (b * TPB + t + 1))
                sp.dma_start(yd[blk * TT + (b * TPB + t)], y[:, t, :]).then_inc(st_y[t], DMA)

            for n in range(2):
                sp.sem_inc(st_y[n], DMA)
            load_rows(0, True)
            for dst, src in ((ln_scale, across(ln_s)), (ln_shift, across(ln_b)), (b1_col, column(b1)), (b2_row, across(b2))):
                sp.dma_start(dst[:, :], src, allow_slow_non_contiguous=True).then_inc(ld_c, DMA)
            for n in range(4):
                load_chunk(n)
            load_rows(1, False)
            for n in range(4, len(chunks)):
                load_chunk(n)
            sp.wait_ge(w_lo, len(chunks))
            for t in range(TT):
                load_t(0, t)

            def body(blk, last):
                if not last:
                    load_rows(blk + 1, False)
                load_m2(blk - 1, 0)
                load_m2(blk - 1, 1)
                for b in range(BPB):
                    for t in range(TPB):
                        store(blk - 1, b, t)
                    for t in range(TPB):
                        load_t(blk, b * TPB + t)
            with sp.Fori(1, NB - 1) as i:
                body(i, False)
            body(NB - 1, True)
            load_m2(NB - 1, 0)
            load_m2(NB - 1, 1)
            for b in range(BPB):
                for t in range(TPB):
                    store(NB - 1, b, t)
            for n in range(2):
                sp.wait_ge(st_y[n], DMA * (B * TPB // 2 + 1))

        @block.gpsimd
        def _(pool):
            def normalise(blk):
                pool.wait_ge(ln_mv, blk + 1)
                pool.tensor_tensor(ve[:, :], mv[:, :, 1], eps[:, :], ALU.add).then_inc(ln_ve, 1)
                pool.wait_ge(ln_ve, blk + 1)
                pool.tensor_tensor(rstd[:, :], ve[:, :], half[:, :], ALU.pow).then_inc(ln_rs, 1)
                wait_apart(pool, ln_rs, blk + 1)
                for t in range(TT):
                    pool.tensor_scalar(x[:, t, :], x[:, t, :], mv[:, t, 0:1], rstd[:, t:t + 1],
                                       ALU.subtract, ALU.mult).then_inc(ln_n, 1)
                    pool.wait_ge(ln_n, blk * TT + (t + 1))
                    pool.tensor_tensor(x[:, t, :], x[:, t, :], ln_scale[:, :], ALU.mult).then_inc(ln_g, 1)
                    pool.wait_ge(ln_g, blk * TT + (t + 1))
                    pool.tensor_tensor(x[:, t, :], x[:, t, :], ln_shift[:, :], ALU.add).then_inc(ln_x, 1)

            def add_bias(blk):
                for t in range(TT):
                    pool.wait_ge(ld_t[t], (blk + 1) * DMA)
                    pool.tensor_tensor(t_sb[:, t, :], t_sb[:, t, :], b2_row[:, :], ALU.add).then_inc(t_bias, 1)

            make_identity(pool, ident, made)
            pool.memset(half[:, :], -0.5).then_inc(half_ok, 1)
            pool.memset(eps[:, :], EPS).then_inc(half_ok, 1)
            pool.wait_ge(half_ok, 2)
            pool.wait_ge(ld_c, n_consts * DMA)
            normalise(0)
            normalise(1)
            add_bias(0)
            with pool.Fori(1, NB - 1) as i:
                normalise(i + 1)
                add_bias(i)
            add_bias(NB - 1)

        @block.tensor
        def _(pe):
            in_bank = [None, None]

            def occupy(unit, bank, blk):
                if in_bank[bank] is not None:
                    wait(pe, *read_out(in_bank[bank], blk))
                in_bank[bank] = unit

            def older():
                for b in range(2):
                    if in_bank[b] is not None:
                        kind, n, rel = in_bank[b]
                        in_bank[b] = kind, n, rel - 1

            def turn(item, blk):
                unit, (bank, _) = item
                occupy(unit, bank, blk)
                n, tb = unit[1], blk + unit[2]
                pe.wait_ge(ln_x, tb * TT + (n + 1))
                for f in range(KT):
                    last = pe.transpose(banks[:, bank, f * P:(f + 1) * P], x[:, n, f * P:(f + 1) * P], ident[:, :])
                last.then_inc(done, 1)

            def hidden(blk, f, first):
                n = blk * FT + f
                if f == 0:
                    pe.wait_ge(x_lo, (blk + 1) * TT)
                if first and f % KT == 0:
                    pe.wait_ge(w_lo, number[(1, KT - 1, f // KT)] + 1)
                wait(pe, h_act, n - 1)
                cols = slice(f * P, (f + 1) * P)
                for t in range(KT):
                    last = product(pe, hb[:, f % 2, :], (w1_h[:, t, cols], w1_l[:, t, cols]),
                                   (xt_h[:, t, :], xt_l[:, t, :]), t == 0, t == KT - 1)
                last.then_inc(h_done, 1)

            def second(blk, f, first):
                if first:
                    pe.wait_ge(w_lo, number[(2, f, 0)] + 1)
                if f == 0:
                    wait(pe, t_ok, blk * TT)
                pe.wait_ge(h_lo, blk * FT + (f + 1))
                for t in range(TT):
                    rows_ = slice(t * P, (t + 1) * P)
                    last = product(pe, acc[:, t, :], (h_h[:, f % 2, rows_], h_l[:, f % 2, rows_]),
                                   (w2_h[:, f, :], w2_l[:, f, :]), f == 0, f == FT - 1)
                last.then_inc(a_done, 1)

            def last_product(item, blk):
                unit, (bank, _) = item
                b, o = unit[1]
                tb = blk + unit[2]
                occupy(unit, bank, blk)
                pe.wait_ge(t_lo, tb * BPB + (b + 1))
                pe.wait_ge(m2_lo, tb * BPB + (b + 2))
                for t in range(TPB):
                    cols = slice(t * S + o * P, t * S + (o + 1) * P)
                    last = product(pe, banks[:, bank, :], (m2_h[:, cols], m2_l[:, cols]), (t_h[:, t, :], t_l[:, t, :]),
                                   t == 0, t == TPB - 1)
                last.then_inc(done, 1)

            def before(items):
                pe.wait_ge(made, 2)
                for item in items:
                    turn(item, -1)
                older()

            def slot(blk, f, first, last, unit, turns):
                if f == 0 and not first:
                    older()
                hidden(blk, f, first)
                for item in turns[:2]:
                    turn(item, blk)
                if f:
                    second(blk, f - 1, first)
                if unit:
                    last_product(unit, blk)
                if f == FT - 1:
                    for item in turns[2:]:
                        turn(item, blk)
                    second(blk, f, first)

            def after(items):
                older()
                for item in items:
                    last_product(item, NB)
            phase(pe, before, slot, after)

        def split_of_t(blk, b):
            return t_sb[:, b * TPB:(b + 1) * TPB, :], t_h[:, :, :], t_l[:, :, :], blk * BPB + (b + 1)

        @block.scalar
        def _(act):
            def split_weights(c):
                n = number[c]
                act.wait_ge(ld_w[n % 4], (n // 4 + 1) * DMA)
                act.activation(parts_of(c)[0], t_sb[:, n % 4, :], ACT.Copy).then_inc(w_hi, 1)

            def turned(item, blk):
                (kind, n, rel), (bank, count) = item
                act.wait_ge(done, count)
                act.activation(xt_h[:, :, n * P:(n + 1) * P], banks[:, bank, :].rearrange("p (f c) -> p f c", f=KT),
                               ACT.Copy).then_inc(x_hi, 1)

            def split_t(blk, b):
                whole, hi, _, n = split_of_t(blk, b)
                act.wait_ge(t_ok, blk * TT + (b + 1) * TPB)
                act.wait_ge(y_ok, (blk + 1) * TT + b * TPB)
                act.activation(hi, whole, ACT.Copy).then_inc(t_hi, 1)
                act.wait_ge(ld_m, n * DMA)
                act.activation(m2_h[:, :], m2[:, :], ACT.Copy).then_inc(m2_hi, 1)

            def before(items):
                for c in first_chunks:
                    split_weights(c)
                for item in items:
                    turned(item, -1)
                act.wait_ge(ld_c, n_consts * DMA)

            def slot(blk, f, first, last, unit, turns):
                if first:
                    for c in slot_chunks[f]:
                        split_weights(c)
                n = blk * FT + f
                act.wait_ge(h_done, n + 1)
                wait(act, h_lo, n - 1)
                act.activation(hf[:, f % 2, :], hb[:, f % 2, :], ACT.Gelu_apprx_tanh, bias=b1_col[:, f:f + 1])\
                   .then_inc(h_act, 1)
                if not first and f in (0, 5):
                    split_t(blk - 1, f // 5)
                for item in turns:
                    turned(item, blk)

            def after(items):
                split_t(NB - 1, 0)
                split_t(NB - 1, 1)
            phase(act, before, slot, after)

        @block.vector
        def _(dve):
            def split_weights(c):
                n = number[c]
                hi, lo = parts_of(c)
                dve.wait_ge(w_hi, n + 1)
                dve.tensor_tensor(lo, t_sb[:, n % 4, :], f32(hi), ALU.subtract).then_inc(w_lo, 1)

            def statistics(blk):
                for t in range(TT):
                    dve.wait_ge(ld_x[t], (blk + 1) * DMA)
                    last = dve.bn_stats(stats[:, t, :], x[:, t, :])
                last.then_inc(ln_st, 1)
                wait_apart(dve, ln_st, blk + 1)
                for t in range(TT):
                    last = dve.bn_aggr(mv[:, t, :], stats[:, t, :])
                last.then_inc(ln_mv, 1)

            def turned(item, blk):
                (kind, n, rel), (bank, count) = item
                rows_ = slice(n * P, (n + 1) * P)
                dve.wait_ge(x_hi, (blk + rel) * TT + (n + 1))
                dve.tensor_tensor(xt_l[:, :, rows_], banks[:, bank, :].rearrange("p (f c) -> p f c", f=KT),
                                  f32(xt_h[:, :, rows_]), ALU.subtract).then_inc(x_lo, 1)

            def split_t(blk, b):
                whole, hi, lo, n = split_of_t(blk, b)
                dve.wait_ge(t_hi, n)
                dve.tensor_tensor(lo, whole, f32(hi), ALU.subtract).then_inc(t_lo, 1)
                dve.wait_ge(m2_hi, n)
                dve.tensor_tensor(m2_l[:, :], m2[:, :], f32(m2_h[:, :]), ALU.subtract).then_inc(m2_lo, 1)

            def last_out(item, blk):
                (kind, (b, o), rel), (bank, count) = item
                tb = blk + rel
                dve.wait_ge(done, count)
                dve.wait_ge(ld_b[b], (tb + 1) * DMA)
                dve.wait_ge(st_y[o], (tb * BPB + (b + 1)) * DMA)
                dve.scalar_tensor_tensor(y[:, o, :], banks[:, bank, :], cb[:, b, o:o + 1], t_sb[:, b * TPB + o, :],
                                         ALU.add, ALU.add).then_inc(y_ok, 1)

            def before(items):
                dve.sem_inc(y_ok, TT)
                dve.sem_inc(m2_lo, 1)
                statistics(0)
                for c in first_chunks:
                    split_weights(c)
                for item in items:
                    turned(item, -1)
                statistics(1)

            def slot(blk, f, first, last, unit, turns):
                if first:
                    for c in slot_chunks[f]:
                        split_weights(c)
                n = blk * FT + f
                dve.wait_ge(h_act, n + 1)
                if not (first and f < 2):
                    dve.wait_ge(a_done, n - 1)
                dve.tensor_copy(h_h[:, f % 2, :], hf[:, f % 2, :]).then_inc(h_hi, 1)
                dve.wait_ge(h_hi, n + 1)
                dve.tensor_tensor(h_l[:, f % 2, :], hf[:, f % 2, :], f32(h_h[:, f % 2, :]), ALU.subtract)\
                   .then_inc(h_lo, 1)
                if f == 1 and not first and not last:
                    statistics(blk + 1)
                if not first and f in (0, 5):
                    split_t(blk - 1, f // 5)
                if unit:
                    last_out(unit, blk)
                for item in turns:
                    turned(item, blk)
                if f == FT - 1:
                    dve.wait_ge(a_done, n + 1)
                    for t in range(TT):
                        dve.wait_ge(t_bias, blk * TT + (t + 1))
                        dve.tensor_tensor(t_sb[:, t, :], acc[:, t, :], t_sb[:, t, :], ALU.add).then_inc(t_ok, 1)

            def after(items):
                split_t(NB - 1, 0)
                for item in items[:2]:
                    last_out(item, NB)
                split_t(NB - 1, 1)
                for item in items[2:]:
                    last_out(item, NB)
            phase(dve, before, slot, after)


def decoder_layer_and_nonlocal(nc, a, out):
    m2t = nc.dram_tensor("m2t", [B, P, TPB * S], F32, kind="Internal").ap()
    cb = nc.dram_tensor("cb", [B, P, TPB], F32, kind="Internal").ap()
    x1 = nc.dram_tensor("x1", [B, S, H], F32, kind="Internal").ap()
    x2 = nc.dram_tensor("x2", [B, S, H], F32, kind="Internal").ap()
    nl = {k[len("L1_xattn_"):]: v for k, v in a.items() if k.startswith("L1_xattn_")}
    d = {k[len("L0_xattn_"):]: v for k, v in a.items() if k.startswith("L0_xattn_")}
    context = a["ctx_2048"]
    nonlocal_phase(nc, {**nl, "ctx": context}, m2t, cb)
    attention_phase(nc, "S", a["x"], None, a["mask_1x1xSxS2_fc1"],
                    [d["w_qkv"][:, c * H:(c + 1) * H] for c in range(3)] + [d["w_ao"]],
                    [d["b_qkv"][c * H:(c + 1) * H] for c in range(3)], d["b_ao"], d["ln1_s"], d["ln1_b"], x1)
    attention_phase(nc, "X", x1, context, a["mask_Bx1xSxS2_ff1"],
                    [d["w_q"], d["w_kv"][:, 0:H], d["w_kv"][:, H:2 * H], d["w_co"]],
                    [d["b_q"], d["b_kv"][0:H], d["b_kv"][H:2 * H]], d["b_co"], d["ln2_s"], d["ln2_b"], x2)
    mlp_phase(nc, x2, d["w1"], d["b1"], d["w2"], d["b2"], d["ln3_s"], d["ln3_b"], m2t, cb, out)


def kernel(**inputs):
    import concourse.bacc as bacc
    from concourse.bass_utils import run_bass_kernel_spmd

    nc = bacc.Bacc("TRN2", target_bir_lowering=False, num_devices=1)
    arrays, aps = {}, {}
    for name, value in inputs.items():
        arrays[name] = np.ascontiguousarray(value)
        aps[name] = nc.dram_tensor(name, arrays[name].shape, mybir.dt.from_np(arrays[name].dtype),
                                   kind="ExternalInput").ap()
    out = nc.dram_tensor("out", [B, S, H], F32, kind="ExternalOutput").ap()
    decoder_layer_and_nonlocal(nc, aps, out)
    return run_bass_kernel_spmd(nc, [arrays], core_ids=[0]).results[0]["out"]
```

```python
from contextlib import ExitStack

import numpy as np
import concourse.bass as bass
import concourse.mybir as mybir

F32 = mybir.dt.float32
F32R = mybir.dt.float32r
ALU = mybir.AluOpType
ACT = mybir.ActivationFunctionType

P = 128
B, S, H = 16, 256, 512
NH, HD = 16, 32
KT = H // P
TPB = S // P
BPB = 2
TOK = BPB * S
TT = TOK // P
NB = B // BPB
HPG = P // HD
NG = BPB * KT
FF = 4 * H
FT = FF // P
CI = 128
EPS = 1e-5
BIG = 3.0e38
DMA = 16


def wait(eng, sem, value):
    if isinstance(value, int) and value <= 0:
        return
    eng.wait_ge(sem, value)


def wait_apart(eng, sem, value):
    eng.wait_ge(sem, 1)
    eng.wait_ge(sem, value)


def f32(ap):
    return ap.bitcast(F32)


def column(ap):
    return ap.rearrange("(t p) -> p t", p=P)


def across(ap):
    n = ap.shape[0]
    return ap.rearrange("(a n) -> a n", a=1).broadcast_to([P, n])


def product(pe, out, stationary, moving, first, last):
    (sh, sl), (mh, ml) = stationary, moving
    pe.matmul(out, sh, mh, start=first, stop=False)
    pe.matmul(out, sh, ml, start=False, stop=False)
    return pe.matmul(out, sl, mh, start=False, stop=last)


class Units:

    def __init__(self):
        self.before, self.k, self.turn, self.per_turn = 0, 0, 0, 0

    def enter(self, turn, per_turn):
        assert per_turn % 2 == 0
        self.before, self.k, self.turn, self.per_turn = self.before + self.k, 0, turn, per_turn

    def leave(self, turns):
        assert self.k == self.per_turn
        self.before, self.k, self.turn = self.before + turns * self.per_turn, 0, 0

    def take(self):
        n = self.before + self.k
        self.k += 1
        return n % 2, self.turn * self.per_turn + (n + 1)


class Room:

    def __init__(self, nc, stack, tag):
        self.nc, self.stack, self.tag, self.all_sems = nc, stack, tag, []

    def sb(self, name, shape, dtype=F32):
        return self.stack.enter_context(self.nc.sbuf_tensor(f"{self.tag}_{name}", shape, dtype))

    def ps(self, name, shape):
        return self.stack.enter_context(self.nc.psum_tensor(f"{self.tag}_{name}", shape, F32))

    def sem(self, name):
        self.all_sems.append(self.stack.enter_context(self.nc.semaphore(f"{self.tag}_{name}")))
        return self.all_sems[-1]

    def sems(self, name, n):
        return [self.sem(f"{name}{k}") for k in range(n)]

    def block(self):
        self.stack.callback(self.clear)
        return self.stack.enter_context(self.nc.Block())

    def clear(self):
        nums = sorted(sem.num for sem in self.all_sems)
        starts = [n for n in nums if n - 1 not in nums]
        stops = [n + 1 for n in nums if n + 1 not in nums]
        for start, stop in zip(starts, stops):
            self.nc.gpsimd.sem_clear(range(start, stop))


def make_identity(pool, ident, made):
    pool.memset(ident[:, :], 0.0).then_inc(made, 1)
    pool.wait_ge(made, 1)
    pool.affine_select(out=ident[:, :], in_=ident[:, :], compare_op=ALU.not_equal, fill=1.0, base=0,
                       pattern=[[-1, P]], channel_multiplier=1).then_inc(made, 1)


def nonlocal_phase(nc, a, m2t_dram, cb_dram):
    OC = S // P
    with ExitStack() as stack:
        r = Room(nc, stack, "N")
        ident = r.sb("ident", [P, P])
        raw_pg = r.sb("raw_pg", [P, 2, S])
        pg_h = r.sb("pg_h", [P, OC, 2 * CI], F32R)
        pg_l = r.sb("pg_l", [P, OC, 2 * CI], F32R)
        pg_bias = r.sb("pg_bias", [P, 2 * CI])
        theta = r.sb("theta", [P, S])
        theta_b = r.sb("theta_b", [P, 1])
        raw_w = r.sb("raw_w", [P, OC, CI])
        w_s = r.sb("w_s", [P, OC, CI])
        w_t = r.sb("w_t", [P, S])
        bn = r.sb("bn", [P, 5, OC])
        ve = r.sb("ve", [P, OC])
        half = r.sb("half", [P, OC])
        inv = r.sb("inv", [P, OC])
        gain = r.sb("gain", [P, OC])
        fix0 = r.sb("fix0", [P, OC])
        fix1 = r.sb("fix1", [P, OC])
        fix = r.sb("fix", [P, OC])
        ctx = r.sb("ctx", [P, 2, OC, H])
        ctx_h = r.sb("ctx_h", [P, 2, OC, H], F32R)
        ctx_l = r.sb("ctx_l", [P, 2, OC, H], F32R)
        pg = r.sb("pg", [P, 2, KT, 2 * CI])
        pgt = r.sb("pgt", [P, 2, CI])
        m1t = r.sb("m1t", [P, 2, S])
        m2t = r.sb("m2t", [P, 2, OC * S])
        cb = r.sb("cb", [P, 2, OC])
        big = r.ps("big", [P, 4, 512])
        small = r.ps("small", [P, 4, 512])

        ld_c, made = r.sem("ld_c"), r.sem("made")
        po, fixed = r.sem("po"), r.sem("fixed")
        pe_prep = r.sem("pe_prep")
        wh_done, wl_done, ws_done, wt_done = (r.sem(n) for n in ("wh_done", "wl_done", "ws_done", "wt_done"))
        ld = r.sems("ld", 2)
        split_h, split_l = r.sem("split_h"), r.sem("split_l")
        mm_pg, mm_1, mm_2, mm_3, mm_b = (r.sem(n) for n in ("mm_pg", "mm_1", "mm_2", "mm_3", "mm_b"))
        ev_pg, ev_1, ev_2, ev_3, ev_b = (r.sem(n) for n in ("ev_pg", "ev_1", "ev_2", "ev_3", "ev_b"))
        st = r.sems("st", 2)
        block = r.block()
        ctx_d = a["ctx"].rearrange("b (t p) n -> b p t n", p=P)
        CONSTS = 12

        def steps(eng, step):
            step(1, 1)
            step(2, 0)
            with eng.Fori(1, B // 2 - 1) as i:
                step(i * 2 + 1, 1)
                step(i * 2 + 2, 0)
            step(B - 1, 1)

        @block.sync
        def _(sp):
            def small_load(dst, src):
                sp.dma_start(dst, src, allow_slow_non_contiguous=True).then_inc(ld_c, DMA)
            small_load(raw_pg[:, 0, :], a["phi_w"])
            small_load(raw_pg[:, 1, :], a["g_w"])
            for b in range(2):
                sp.dma_start(ctx[:, b, :, :], ctx_d[b]).then_inc(ld[b], DMA)
            small_load(theta[:, :], a["theta_w"])
            small_load(raw_w[:, :, :], a["w_w"].rearrange("(t p) c -> p t c", p=P))
            for k, n in enumerate(("bn_gamma", "bn_beta", "bn_mean", "bn_var", "w_b")):
                small_load(bn[:, k, :], column(a[n]))
            small_load(pg_bias[:, 0:CI], across(a["phi_b"]))
            small_load(pg_bias[:, CI:], across(a["g_b"]))
            sp.dma_start(theta_b[:, :], column(a["theta_b"]), allow_slow_non_contiguous=True).then_inc(ld_c, DMA)

            def load(b, par):
                wait(sp, split_l, b - 1)
                sp.dma_start(ctx[:, par, :, :], ctx_d[b]).then_inc(ld[par], DMA)

            def store(b, par):
                sp.wait_ge(ev_3, b + 1)
                sp.dma_start(m2t_dram[b], m2t[:, par, :]).then_inc(st[par], DMA)
                sp.wait_ge(ev_b, b + 1)
                sp.dma_start(cb_dram[b], cb[:, par, :]).then_inc(st[par], DMA)
            load(2, 0)
            with sp.Fori(1, B // 2 - 1) as i:
                load(i * 2 + 1, 1)
                store(i * 2 - 2, 0)
                load(i * 2 + 2, 0)
                store(i * 2 - 1, 1)
            load(B - 1, 1)
            for n in range(4):
                store(B - 4 + n, n % 2)
            for par in range(2):
                sp.wait_ge(st[par], 2 * DMA * (B // 2))

        @block.gpsimd
        def _(pool):
            make_identity(pool, ident, made)
            pool.memset(half[:, :], -0.5).then_inc(po, 1)
            pool.wait_ge(ld_c, CONSTS * DMA)
            pool.wait_ge(po, 1)
            pool.tensor_scalar(ve[:, :], bn[:, 3, :], EPS, None, ALU.add).then_inc(po, 1)
            pool.wait_ge(po, 2)
            pool.tensor_tensor(inv[:, :], ve[:, :], half[:, :], ALU.pow).then_inc(po, 1)

        @block.tensor
        def _(pe):
            pe.wait_ge(made, 2)
            pe.wait_ge(ld_c, CONSTS * DMA)
            for w in range(2):
                for t in range(OC):
                    last = pe.transpose(big[:, t, w * CI:(w + 1) * CI], raw_pg[:, w, t * P:(t + 1) * P], ident[:, :])
            last.then_inc(pe_prep, 1)
            pe.wait_ge(ws_done, OC)
            for t in range(OC):
                last = pe.transpose(small[:, 0, t * P:(t + 1) * P], w_s[:, t, :], ident[:, :])
            last.then_inc(pe_prep, 1)
            pe.wait_ge(wl_done, 1)
            pe.wait_ge(wt_done, 1)

            def phi_g(b, par, m):
                if m == 0:
                    pe.wait_ge(split_l, b + 1)
                    wait(pe, ev_pg, 2 * b - 2)
                out = big[:, 2 * par + m // 2, (m % 2) * S:(m % 2 + 1) * S]
                for t in range(OC):
                    cols = slice(m * P, (m + 1) * P)
                    last = product(pe, out, (ctx_h[:, par, t, cols], ctx_l[:, par, t, cols]),
                                   (pg_h[:, t, :], pg_l[:, t, :]), t == 0, t == OC - 1)
                if m % 2:
                    last.then_inc(mm_pg, 1)

            def chain_1(b, par):
                pe.wait_ge(ev_pg, 2 * b + 2)
                for m in range(KT):
                    last = pe.matmul(small[:, 0, 0:CI], pg[:, par, m, CI:], pg[:, par, m, 0:CI],
                                     start=(m == 0), stop=(m == KT - 1))
                last.then_inc(mm_1, 1)

            def chain_2(b, par):
                pe.wait_ge(ev_1, b + 1)
                pe.matmul(small[:, 1, 0:S], pgt[:, par, :], w_t[:, :], start=True, stop=True).then_inc(mm_2, 1)

            def chain_3(b, par):
                pe.wait_ge(ev_2, b + 1)
                wait(pe, ev_3, b)
                for t in range(OC):
                    last = pe.matmul(small[:, 2, t * S:(t + 1) * S], theta[:, t * P:(t + 1) * P], m1t[:, par, :],
                                     start=True, stop=True)
                last.then_inc(mm_3, 1)
                wait(pe, ev_b, b)
                for t in range(OC):
                    last = pe.matmul(small[:, 3, t:t + 1], m1t[:, par, t * P:(t + 1) * P], theta_b[:, :],
                                     start=True, stop=True)
                last.then_inc(mm_b, 1)

            def step(b, par):
                phi_g(b, par, 0)
                phi_g(b, par, 1)
                chain_1(b - 1, 1 - par)
                phi_g(b, par, 2)
                chain_2(b - 1, 1 - par)
                phi_g(b, par, 3)
                chain_3(b - 1, 1 - par)
            for m in range(KT):
                phi_g(0, 0, m)
            steps(pe, step)
            chain_1(B - 1, 1)
            chain_2(B - 1, 1)
            chain_3(B - 1, 1)

        @block.scalar
        def _(act):
            act.wait_ge(pe_prep, 1)
            act.activation(pg_h[:, :, :], big[:, 0:OC, 0:2 * CI], ACT.Copy).then_inc(wh_done, 1)

            def hi(b, par):
                act.wait_ge(ld[par], (b - par) * (DMA // 2) + DMA)
                wait(act, mm_pg, 2 * b - 2)
                act.activation(ctx_h[:, par, :, :], ctx[:, par, :, :], ACT.Copy).then_inc(split_h, 1)

            def out(b, par):
                act.wait_ge(mm_1, b + 1)
                act.activation(pgt[:, par, :], small[:, 0, 0:CI], ACT.Copy).then_inc(ev_1, 1)
                act.wait_ge(mm_2, b + 1)
                act.activation(m1t[:, par, :], small[:, 1, 0:S], ACT.Copy).then_inc(ev_2, 1)
                act.wait_ge(mm_3, b + 1)
                wait(act, st[par], (b - par) * DMA)
                act.activation(m2t[:, par, :], small[:, 2, :], ACT.Copy).then_inc(ev_3, 1)

            def step(b, par):
                if not (isinstance(b, int) and b == B - 1):
                    hi(b + 1, 1 - par)
                out(b - 1, 1 - par)
            hi(0, 0)
            hi(1, 1)
            steps(act, step)
            out(B - 1, 1)

        @block.vector
        def _(dve):
            dve.wait_ge(po, 3)
            n = 0

            def link(ins):
                nonlocal n
                n += 1
                ins.then_inc(fixed, 1)
                dve.wait_ge(fixed, n)
            link(dve.tensor_tensor(gain[:, :], bn[:, 0, :], inv[:, :], ALU.mult))
            link(dve.tensor_tensor(fix0[:, :], bn[:, 4, :], bn[:, 2, :], ALU.subtract))
            link(dve.tensor_tensor(fix1[:, :], fix0[:, :], gain[:, :], ALU.mult))
            link(dve.tensor_tensor(fix[:, :], fix1[:, :], bn[:, 1, :], ALU.add))
            for t in range(OC):
                last = dve.tensor_scalar(w_s[:, t, :], raw_w[:, t, :], gain[:, t:t + 1], 1.0 / H, ALU.mult, ALU.mult)
                last.then_inc(ws_done, 1)
            dve.wait_ge(wh_done, 1)
            dve.tensor_tensor(pg_l[:, :, :], big[:, 0:OC, 0:2 * CI], f32(pg_h[:, :, :]), ALU.subtract).then_inc(wl_done, 1)
            dve.wait_ge(pe_prep, 2)
            dve.tensor_copy(w_t[:, :], small[:, 0, 0:S]).then_inc(wt_done, 1)

            def lo(b, par):
                dve.wait_ge(split_h, b + 1)
                wait(dve, mm_pg, 2 * b - 2)
                dve.tensor_tensor(ctx_l[:, par, :, :], ctx[:, par, :, :], f32(ctx_h[:, par, :, :]), ALU.subtract)\
                   .then_inc(split_l, 1)

            def add_bias(b, par):
                for n in range(2):
                    dve.wait_ge(mm_pg, 2 * b + (n + 1))
                    wait(dve, mm_1, b - 1)
                    dve.tensor_tensor(pg[:, par, 2 * n:2 * n + 2, :],
                                      big[:, 2 * par + n, :].rearrange("p (m c) -> p m c", m=2),
                                      pg_bias[:, :].unsqueeze(1).to_broadcast([P, 2, 2 * CI]), ALU.add).then_inc(ev_pg, 1)

            def bias(b, par):
                dve.wait_ge(mm_b, b + 1)
                wait(dve, st[par], (b - par) * DMA)
                dve.tensor_tensor(cb[:, par, :], small[:, 3, 0:OC], fix[:, :], ALU.add).then_inc(ev_b, 1)

            def step(b, par):
                if not (isinstance(b, int) and b == B - 1):
                    lo(b + 1, 1 - par)
                add_bias(b, par)
                bias(b - 1, 1 - par)
            lo(0, 0)
            lo(1, 1)
            add_bias(0, 0)
            steps(dve, step)
            bias(B - 1, 1)


def attention_phase(nc, tag, rows, context, mask, weights, biases, out_bias, ln_s, ln_b, out):
    cross = context is not None
    with ExitStack() as stack:
        r = Room(nc, stack, tag)
        ident = r.sb("ident", [P, P])
        w_h = r.sb("w_h", [P, KT, 4 * H], F32R)
        w_l = r.sb("w_l", [P, KT, 4 * H], F32R)
        lns = r.sb("lns", [P, KT])
        lns_q = r.sb("lns_q", [P, KT])
        lnb = r.sb("lnb", [P, KT])
        bias_in = r.sb("bias_in", [P, 3, KT])
        bias_sum = r.sb("bias_sum", [P, 3, KT])
        bias_q = r.sb("bias_q", [P, KT])
        o_bias = r.sb("o_bias", [P, H])
        half = r.sb("half", [P, TT])
        eps = r.sb("eps", [P, TT])
        big_one = r.sb("big_one", [P, 2])
        n_mask = BPB if cross else 1
        mk = r.sb("mk", [P, n_mask, TPB, S])
        ma = r.sb("ma", [P, n_mask, TPB, S])
        x = r.sb("x", [P, TT, H])
        stats = r.sb("stats", [P, TT, 6])
        mv = r.sb("mv", [P, TT, 2])
        ve = r.sb("ve", [P, TT])
        rstd = r.sb("rstd", [P, TT])
        xt_h = r.sb("xt_h", [P, KT, TOK], F32R)
        xt_l = r.sb("xt_l", [P, KT, TOK], F32R)
        if cross:
            e = r.sb("e", [P, 2, H])
            et_h = r.sb("et_h", [P, KT, TOK], F32R)
            et_l = r.sb("et_l", [P, KT, TOK], F32R)
        else:
            et_h, et_l = xt_h, xt_l
        q_h = r.sb("q_h", [P, KT, TOK], F32R)
        q_l = r.sb("q_l", [P, KT, TOK], F32R)
        k_h = r.sb("k_h", [P, KT, TOK], F32R)
        k_l = r.sb("k_l", [P, KT, TOK], F32R)
        v = r.sb("v", [P, TT, H])
        p = r.sb("p", [P, 2, HPG, TPB, S])
        nmax = r.sb("nmax", [P, 2, HPG, TPB])
        rsum = r.sb("rsum", [P, 2, HPG, TPB])
        rinv = r.sb("rinv", [P, 2, HPG, TPB])
        rwide = r.sb("rwide", [P, 2, TPB, P])
        pt = r.sb("pt", [P, HPG, TPB, S])
        raws = [a_.rearrange("p j t s -> p j (t s)") for a_ in (p[:, 1, :, :, :], p[:, 0, :, :, :], pt[:, :, :, :])]
        rt = r.sb("rt", [P, S])
        cx = r.sb("cx", [P, S])
        ct_h = r.sb("ct_h", [P, KT, TOK], F32R)
        ct_l = r.sb("ct_l", [P, KT, TOK], F32R)
        res = r.sb("res", [P, 2, H])
        sc = r.ps("sc", [P, HPG, 512])
        tp = r.ps("tp", [P, 2, 512])
        banks = r.ps("banks", [P, 2, 512])

        made, half_ok = r.sem("made"), r.sem("half_ok")
        ld_c, ld_ln = r.sem("ld_c"), r.sem("ld_ln")
        ld_w = [r.sems(f"ld_w{c}_", KT) for c in range(3)]
        ld_x, ld_e = r.sems("ld_x", TT), (r.sems("ld_e", 2) if cross else None)
        ld_r, st_y, ld_m = r.sems("ld_r", 2), r.sems("st_y", 2), r.sems("ld_m", n_mask)
        w_hi, w_lo = r.sem("w_hi"), r.sem("w_lo")
        folded, bias_ok, bias_q_ok, lns_ok = (r.sem(n) for n in ("folded", "bias_ok", "bias_q_ok", "lns_ok"))
        ln_st, ln_mv, ln_ve, ln_rs, ln_x = (r.sem(n) for n in ("ln_st", "ln_mv", "ln_ve", "ln_rs", "ln_x"))
        done = r.sem("done")
        x_hi, x_lo, e_hi, e_lo = (r.sem(n) for n in ("x_hi", "x_lo", "e_hi", "e_lo"))
        q_hi, q_lo, k_hi, k_lo, v_ok = (r.sem(n) for n in ("q_hi", "q_lo", "k_hi", "k_lo", "v_ok"))
        scored, masked, biased, exped = (r.sem(n) for n in ("scored", "masked", "biased", "exped"))
        inv_ok, wide_ok = r.sem("inv_ok"), r.sem("wide_ok")
        turned, pt_ok = r.sem("turned"), r.sem("pt_ok")
        rt_ok, cx_ok, c_hi, c_lo = (r.sem(n) for n in ("rt_ok", "cx_ok", "c_hi", "c_lo"))
        res_ok, y_ok, m_ok, m1_ok = (r.sem(n) for n in ("res_ok", "y_ok", "m_ok", "m1_ok"))
        block = r.block()

        scale = float(HD) ** -0.5
        xd = rows.rearrange("b (t p) n -> (b t) p n", p=P)
        ed = context.rearrange("b (t p) n -> (b t) p n", p=P) if cross else None
        yd = out.rearrange("b (t p) n -> (b t) p n", p=P)
        md = mask.rearrange("b a (t p) n -> (b a) p t n", p=P)
        fold = [True, not cross, not cross]
        n_consts = 3 + 1
        src_lo = e_lo if cross else x_lo

        def factor(c, t):
            if c == 0:
                return lns_q[:, t:t + 1]
            return lns[:, t:t + 1] if c < 3 and fold[c] else 1.0

        order = [1, 0, 2, 3] if cross else [0, 1, 2, 3]
        place = {c: n for n, c in enumerate(order)}
        raw_of = lambda c: (raws[place[c] % 3], ld_w[place[c] % 3], (place[c] // 3 + 1) * DMA)

        def in_slot(g, first, last):
            pre, post = [
                ([("v", 0, 0)], [("o", 0, -1), ("e", 0, 1)]),
                ([("o", 1, -1), ("v", 1, 0)], [("v", 2, 0), ("e", 1, 1)]),
                ([("x", 0, 1), ("v", 3, 0)], [("o", 2, -1), ("x", 1, 1), ("e", 2, 1)]),
                ([("x", 2, 1), ("x", 3, 1)], [("o", 3, -1)]),
                ([("e", 3, 1), ("q", 0, 1)], [("k", 0, 1)]),
                ([("q", 1, 1)], [("k", 1, 1)]),
                ([("q", 2, 1)], [("k", 2, 1)]),
                ([("q", 3, 1)], [("k", 3, 1)]),
            ][g]
            if first and g < 2:
                post = post + [("q", g + 2, 0)] + ([] if cross else [("k", g + 2, 0)])
            if last and g in (5, 6):
                post = post + [("o", g - 5, 0)]
            runs = lambda u: not (first and u[2] < 0) and not (last and u[2] > 0) and (cross or u[0] != "e")
            return list(filter(runs, pre)), list(filter(runs, post))

        def ends_with(pre):
            sizes = [1 if unit[0] in "xe" else KT for unit, _ in pre]
            ends = [sum(sizes[:n + 1]) for n in range(len(sizes))]
            return [next(j for j in range(HPG) if end <= (j + 1) * sum(sizes) // HPG) for end in ends]

        PER_BLOCK = NG + sum(len(a_) + len(b_) for a_, b_ in (in_slot(g, False, False) for g in range(NG)))
        X, E, Q, K_ = ([(c, n, 1) for n in range(4)] for c in "xeqk")
        if cross:
            BEFORE = [*E[:2], "split 1", "statistics", *E[2:], "normalise", "bias 1", *K_[:2], *X, "split 0", "fold 0",
                      "bias 0", "bias 2", Q[0], "scores", "split 2", Q[1], K_[2], "split 3", "maxima", K_[3]]
        else:
            BEFORE = ["statistics", "split 0", "normalise", *X, "fold 0", "bias 0", "split 1", Q[0], "fold 1", "bias 1",
                      "fold 2", "bias 2", K_[0], "scores", "split 2", K_[1], Q[1], "split 3", "maxima"]
        AFTER = [("o", 2, -1), ("o", 3, -1)]

        def read_out(unit, blk):
            kind, n, rel = unit
            if kind == "pv":
                return cx_ok, (blk + rel) * NG + n
            sem, per = {"x": (x_lo, TT), "e": (e_lo, TT), "q": (q_lo, KT), "k": (k_lo, KT), "v": (v_ok, TT),
                        "o": (y_ok, TT)}[kind]
            return sem, (blk + rel) * per + (n + 1)

        def phase(eng, before, slot, after):
            units = Units()
            for step in BEFORE:
                if isinstance(step, tuple):
                    before["unit"]((step, units.take()))
                else:
                    name, *part = step.split()
                    if name in before:
                        before[name](*map(int, part))

            def body(blk, first, last):
                for g in range(NG):
                    pre, post = in_slot(g, first, last)
                    pre = [(u, units.take()) for u in pre]
                    pv = None if first and g == 0 else units.take()
                    slot(blk, g, first, last, pre, pv, [(u, units.take()) for u in post])
            body(0, True, False)
            with eng.Fori(1, NB - 1) as i:
                units.enter(i - 1, PER_BLOCK)
                body(i, False, False)
            units.leave(NB - 2)
            body(NB - 1, False, True)
            after(units.take(), [(u, units.take()) for u in AFTER])

        @block.sync
        def _(sp):
            def const(dst, src, sem=ld_c):
                sp.dma_start(dst, src, allow_slow_non_contiguous=True).then_inc(sem, DMA)

            def load_weights(c):
                raw, loaded, _ = raw_of(c)
                for t in range(KT):
                    if place[c] == 3:
                        sp.wait_ge(w_lo, t + 1)
                        if fold[order[0]]:
                            sp.wait_ge(folded, 1)
                    sp.dma_start(raw[:, t, :], weights[c][t * P:(t + 1) * P, :]).then_inc(loaded[t], DMA)

            def load_rows(blk, first):
                for t in range(TT):
                    if not first:
                        sp.wait_ge(x_lo, (blk - 1) * TT + (t + 1))
                    sp.dma_start(x[:, t, :], xd[blk * TT + t]).then_inc(ld_x[t], DMA)

            def load_context(blk, t):
                wait(sp, e_lo, blk * TT + (t - 1))
                sp.dma_start(e[:, t % 2, :], ed[blk * TT + t]).then_inc(ld_e[t % 2], DMA)

            def load_mask(blk, b):
                sp.wait_ge(biased, ((blk - 1) * NG + (b + 1) * KT) * HPG * TPB)
                sp.dma_start(mk[:, b, :, :], md[blk * BPB + b]).then_inc(ld_m[b], DMA)

            def load_res(blk, t):
                wait(sp, st_y[t % 2], (blk * 2 + t // 2) * DMA)
                sp.dma_start(res[:, t % 2, :], xd[blk * TT + t]).then_inc(ld_r[t % 2], DMA)

            def store(blk, t):
                sp.wait_ge(y_ok, blk * TT + (t + 1))
                sp.dma_start(yd[blk * TT + t], res[:, t % 2, :]).then_inc(st_y[t % 2], DMA)

            if cross:
                load_context(0, 0)
                load_context(0, 1)
            else:
                load_rows(0, True)
            const(lns[:, :], column(ln_s), ld_ln)
            const(lnb[:, :], column(ln_b), ld_ln)
            load_weights(order[0])
            if cross:
                load_rows(0, True)
                load_context(0, 2)
                load_context(0, 3)
            for c in range(3):
                const(bias_in[:, c, :], column(biases[c]))
            const(o_bias[:, :], across(out_bias))
            load_weights(order[1])
            load_weights(order[2])
            for b in range(n_mask):
                sp.dma_start(mk[:, b, :, :], md[b]).then_inc(ld_m[b], DMA)
            load_weights(order[3])
            load_res(0, 0)
            load_res(0, 1)

            def body(blk, first, last):
                if not last:
                    load_rows(blk + 1, False)
                    if cross:
                        load_context(blk + 1, 0)
                        load_context(blk + 1, 1)
                if cross and not first:
                    load_mask(blk, 1)
                if not first:
                    store(blk - 1, 0)
                    load_res(blk - 1, 2)
                if cross and not last:
                    load_context(blk + 1, 2)
                if not first:
                    store(blk - 1, 1)
                    load_res(blk - 1, 3)
                if cross and not last:
                    load_context(blk + 1, 3)
                if not first:
                    store(blk - 1, 2)
                    load_res(blk, 0)
                    store(blk - 1, 3)
                    load_res(blk, 1)
                if cross and not last:
                    load_mask(blk + 1, 0)
            body(0, True, False)
            with sp.Fori(1, NB - 1) as i:
                body(i, False, False)
            body(NB - 1, False, True)
            store(NB - 1, 0)
            load_res(NB - 1, 2)
            store(NB - 1, 1)
            load_res(NB - 1, 3)
            store(NB - 1, 2)
            store(NB - 1, 3)
            for n in range(2):
                sp.wait_ge(st_y[n], DMA * (B * TPB // 2))

        @block.gpsimd
        def _(pool):
            def deviations(blk):
                pool.wait_ge(ln_mv, blk + 1)
                pool.tensor_tensor(ve[:, :], mv[:, :, 1], eps[:, :], ALU.add).then_inc(ln_ve, 1)
                pool.wait_ge(ln_ve, blk + 1)
                pool.tensor_tensor(rstd[:, :], ve[:, :], half[:, :], ALU.pow).then_inc(ln_rs, 1)

            def add_bias(blk, t):
                pool.wait_ge(ld_r[t % 2], (blk * 2 + (t // 2 + 1)) * DMA)
                pool.tensor_tensor(res[:, t % 2, :], res[:, t % 2, :], o_bias[:, :], ALU.add).then_inc(res_ok, 1)

            def addend(blk, b):
                n = blk * n_mask + (b + 1)
                whole = lambda c: big_one[:, c:c + 1].unsqueeze(2).to_broadcast([P, TPB, S])
                pool.wait_ge(ld_m[b], (blk + 1) * DMA)
                pool.tensor_tensor(ma[:, b, :, :], mk[:, b, :, :], whole(0), ALU.subtract).then_inc(m1_ok, 1)
                pool.wait_ge(m1_ok, n)
                pool.tensor_tensor(ma[:, b, :, :], ma[:, b, :, :], whole(1), ALU.mult).then_inc(m_ok, 1)

            make_identity(pool, ident, made)
            for tile, value in ((half[:, :], -0.5), (eps[:, :], EPS), (big_one[:, 0:1], 1.0), (big_one[:, 1:2], 10000.0)):
                pool.memset(tile, value).then_inc(half_ok, 1)
            pool.wait_ge(half_ok, 4)
            deviations(0)
            for b in range(n_mask):
                addend(0, b)
            pool.wait_ge(ld_c, n_consts * DMA)
            add_bias(0, 0)
            add_bias(0, 1)

            def body(blk, first, last):
                if cross and not first:
                    addend(blk, 1)
                if not last:
                    deviations(blk + 1)
                if not first:
                    add_bias(blk - 1, 2)
                    add_bias(blk - 1, 3)
                    add_bias(blk, 0)
                    add_bias(blk, 1)
                if cross and not last:
                    addend(blk + 1, 0)
            body(0, True, False)
            with pool.Fori(1, NB - 1) as i:
                body(i, False, False)
            body(NB - 1, False, True)
            add_bias(NB - 1, 2)
            add_bias(NB - 1, 3)

        @block.tensor
        def _(pe):
            in_bank = [None, None]

            def occupy(unit, bank, blk):
                if in_bank[bank] is not None:
                    wait(pe, *read_out(in_bank[bank], blk))
                in_bank[bank] = unit

            def fold_bias(c):
                if not fold[c]:
                    return
                raw, loaded, count = raw_of(c)
                pe.wait_ge(ld_ln, 2 * DMA)
                for t in range(KT):
                    pe.wait_ge(loaded[t], count)
                for f in range(KT):
                    for t in range(KT):
                        last = pe.matmul(sc[:, c, f:f + 1], raw[:, t, f * P:(f + 1) * P],
                                         lnb[:, t:t + 1], start=(t == 0), stop=(t == KT - 1))
                last.then_inc(folded, 1)

            def steps_of(item, blk, first):
                unit, (bank, _) = item
                kind, n, rel = unit
                tb = blk + rel
                o = banks[:, bank, :]

                def transposes():
                    occupy(unit, bank, blk)
                    if kind == "x":
                        pe.wait_ge(ln_x, tb * TT + (n + 1))
                    else:
                        pe.wait_ge(ld_e[n % 2], (tb * 2 + (n // 2 + 1)) * DMA)
                    src = x[:, n, :] if kind == "x" else e[:, n % 2, :]
                    for f in range(KT):
                        last = pe.transpose(o[:, f * P:(f + 1) * P], src[:, f * P:(f + 1) * P], ident[:, :])
                    last.then_inc(done, 1)
                if kind in "xe":
                    return [transposes]
                cols = slice(n * P, (n + 1) * P)
                part = "qkvo".index(kind)
                wcols = slice(part * H, (part + 1) * H) if kind in "vo" else slice(part * H + n * P, part * H + (n + 1) * P)
                sh, sl = {"q": (xt_h, xt_l), "k": (et_h, et_l), "v": (et_h, et_l), "o": (ct_h, ct_l)}[kind]

                def step(t):
                    if t == 0:
                        occupy(unit, bank, blk)
                        if first:
                            pe.wait_ge(w_lo, (place[part] + 1) * KT)
                        if kind == "q":
                            pe.wait_ge(x_lo, (tb + 1) * TT)
                        elif kind == "k":
                            pe.wait_ge(src_lo, (tb + 1) * TT)
                        elif kind == "v":
                            pe.wait_ge(src_lo, tb * TT + (n + 1))
                        else:
                            pe.wait_ge(c_lo, tb * NG + (n // TPB + 1) * KT)
                    w = (w_h[:, t, wcols], w_l[:, t, wcols])
                    if kind in "qk":
                        last = product(pe, o, w, (sh[:, t, :], sl[:, t, :]), t == 0, t == KT - 1)
                    else:
                        last = product(pe, o, (sh[:, t, cols], sl[:, t, cols]), w, t == 0, t == KT - 1)
                    if t == KT - 1:
                        last.then_inc(done, 1)
                return [lambda t=t: step(t) for t in range(KT)]

            def run(items, blk, first):
                for item in items:
                    for s in steps_of(item, blk, first):
                        s()

            def scores(blk, g):
                b, f = g // KT, g % KT
                grp = blk * NG + g
                pe.wait_ge(q_lo, blk * KT + (f + 1))
                pe.wait_ge(k_lo, blk * KT + (f + 1))
                wait(pe, masked, grp)
                for t in range(TPB):
                    rows_, keys = slice(b * S + t * P, b * S + (t + 1) * P), slice(b * S, (b + 1) * S)
                    for n, (qp, kp) in enumerate(((q_h, k_h), (q_h, k_l), (q_l, k_h))):
                        for j in range(HPG):
                            rr = slice(j * HD, (j + 1) * HD)
                            last = pe.matmul(sc[:, j, t * S:(t + 1) * S], qp[rr, f, rows_], kp[rr, f, keys],
                                             start=(n == 0), stop=(n == 2))
                last.then_inc(scored, 1)

            def turn(blk, g, j):
                grp = blk * NG + g
                pe.wait_ge(exped, grp * HPG * TPB + (j + 1) * TPB)
                wait(pe, pt_ok, grp * HPG + (j - 1))
                for t in range(TPB):
                    for c in range(TPB):
                        last = pe.transpose(tp[:, j % 2, c * S + t * P:c * S + (t + 1) * P],
                                            p[:, g % 2, j, t, c * P:(c + 1) * P], ident[:, :])
                last.then_inc(turned, 1)

            def weigh(blk, g, bank, now, rel):
                b, f = g // KT, g % KT
                grp = blk * NG + g
                occupy(("pv", g + 1, rel), bank, now)
                pe.wait_ge(wide_ok, grp + 1)
                for t in range(TPB):
                    pe.transpose(banks[:, bank, S + t * P:S + (t + 1) * P], rwide[:, g % 2, t, :], ident[:, :])
                pe.wait_ge(pt_ok, (grp + 1) * HPG)
                pe.wait_ge(v_ok, blk * TT + (b + 1) * TPB)
                for c in range(TPB):
                    for j in range(HPG):
                        rr = slice(j * HD, (j + 1) * HD)
                        last = pe.matmul(banks[rr, bank, 0:S], v[:, b * TPB + c, f * P + j * HD:f * P + (j + 1) * HD],
                                         pt[:, j, c, :], start=(c == 0), stop=(c == TPB - 1))
                last.then_inc(done, 1)

            def first_scores():
                pe.wait_ge(bias_ok, 3)
                scores(0, 0)

            def older():
                for b in range(2):
                    kind, n, rel = in_bank[b]
                    in_bank[b] = kind, n, rel - 1

            pe.wait_ge(made, 2)
            before = {"unit": lambda item: run([item], -1, True), "fold": fold_bias, "scores": first_scores}

            def slot(blk, g, first, last, pre, pv, post):
                if g == 0:
                    older()
                pb, pg, rel = (blk, g - 1, 0) if g else (blk - 1, NG - 1, -1)
                steps = [s for item in pre for s in steps_of(item, blk, first)]
                for j in range(HPG):
                    if pv is not None:
                        turn(pb, pg, j)
                    for s in steps[j * len(steps) // HPG:(j + 1) * len(steps) // HPG]:
                        s()
                if g + 1 < NG:
                    scores(blk, g + 1)
                elif not last:
                    scores(blk + 1, 0)
                if pv is not None:
                    weigh(pb, pg, pv[0], blk, rel)
                run(post, blk, first)

            def after(pv, items):
                older()
                for j in range(HPG):
                    turn(NB - 1, NG - 1, j)
                weigh(NB - 1, NG - 1, pv[0], NB, -1)
                run(items, NB, False)
            phase(pe, before, slot, after)

        @block.scalar
        def _(act):
            def split_weights(c):
                raw, loaded, count = raw_of(c)
                if c == order[0]:
                    act.wait_ge(lns_ok, 1)
                for t in range(KT):
                    act.wait_ge(loaded[t], count)
                    act.activation(w_h[:, t, c * H:(c + 1) * H], raw[:, t, :], ACT.Copy,
                                   scale=factor(c, t)).then_inc(w_hi, 1)

            def read(item, blk, first):
                (kind, n, rel), (bank, count) = item
                o = banks[:, bank, :]
                if kind == "o":
                    return
                act.wait_ge(done, count)
                if kind in "xe":
                    dst, sem = (xt_h, x_hi) if kind == "x" else (et_h, e_hi)
                    act.activation(dst[:, :, n * P:(n + 1) * P], o.rearrange("p (f c) -> p f c", f=KT), ACT.Copy)\
                       .then_inc(sem, 1)
                elif kind in "qk":
                    if first and kind == "q":
                        act.wait_ge(bias_q_ok, 1)
                    elif first:
                        act.wait_ge(bias_ok, place[1] + 1)
                    dst, bias, sem = (q_h, bias_q, q_hi) if kind == "q" else (k_h, bias_sum[:, 1, :], k_hi)
                    act.activation(dst[:, n, :], o, ACT.Identity, bias=bias[:, n:n + 1]).then_inc(sem, 1)
                else:
                    act.activation(v[:, n, :], o, ACT.Copy).then_inc(v_ok, 1)

            def exponentials(blk, g, j):
                grp = blk * NG + g
                for t in range(TPB):
                    act.wait_ge(biased, grp * HPG * TPB + (j * TPB + t + 1))
                    act.activation(p[:, g % 2, j, t, :], p[:, g % 2, j, t, :], ACT.Exp, scale=-1.0,
                                   bias=nmax[:, g % 2, j, t:t + 1], accum_out=rsum[:, g % 2, j, t:t + 1])\
                       .then_inc(exped, 1)

            def turned_out(blk, g, j):
                grp = blk * NG + g
                act.wait_ge(turned, grp * HPG + (j + 1))
                act.activation(pt[:, j, :, :], tp[:, j % 2, :].rearrange("p (c s) -> p c s", c=TPB), ACT.Copy)\
                   .then_inc(pt_ok, 1)

            def weighed(blk, g, pv):
                b, f = g // KT, g % KT
                grp = blk * NG + g
                bank, count = pv
                act.wait_ge(done, count)
                wait(act, cx_ok, grp)
                act.activation(rt[:, :], banks[:, bank, S:2 * S], ACT.Copy).then_inc(rt_ok, 1)
                act.wait_ge(cx_ok, grp + 1)
                act.activation(ct_h[:, f, b * S:(b + 1) * S], cx[:, :], ACT.Identity, bias=bias_sum[:, 2, f:f + 1])\
                   .then_inc(c_hi, 1)

            before = {"unit": lambda item: read(item, -1, True), "split": split_weights}

            def slot(blk, g, first, last, pre, pv, post):
                pb, pg = (blk, g - 1) if g else (blk - 1, NG - 1)
                if pv is not None:
                    turned_out(pb, pg, 0)
                for j in range(HPG):
                    if pv is not None and j + 1 < HPG:
                        turned_out(pb, pg, j + 1)
                    exponentials(blk, g, j)
                    for item, head in zip(pre, ends_with(pre)):
                        if j == min(head, HPG - 2):
                            read(item, blk, False)
                if pv is not None:
                    weighed(pb, pg, pv)
                for item in post:
                    read(item, blk, False)

            def after(pv, items):
                for j in range(HPG):
                    turned_out(NB - 1, NG - 1, j)
                weighed(NB - 1, NG - 1, pv)
            phase(act, before, slot, after)

        @block.vector
        def _(dve):
            def split_weights(c):
                raw = raw_of(c)[0]
                if c == order[0]:
                    dve.wait_ge(ld_ln, 2 * DMA)
                    dve.tensor_scalar(lns_q[:, :], lns[:, :], scale, None, ALU.mult).then_inc(lns_ok, 1)
                    dve.wait_ge(lns_ok, 1)
                for t in range(KT):
                    dve.wait_ge(w_hi, place[c] * KT + t + 1)
                    hi, lo = f32(w_h[:, t, c * H:(c + 1) * H]), w_l[:, t, c * H:(c + 1) * H]
                    if c < 3 and fold[c]:
                        dve.scalar_tensor_tensor(lo, raw[:, t, :], factor(c, t), hi, ALU.mult, ALU.subtract)\
                           .then_inc(w_lo, 1)
                    else:
                        dve.tensor_tensor(lo, raw[:, t, :], hi, ALU.subtract).then_inc(w_lo, 1)

            def biases_of(c):
                dve.wait_ge(ld_c, n_consts * DMA)
                if fold[c]:
                    dve.wait_ge(folded, sum(fold[d] for d in order[:place[c] + 1]))
                    dve.tensor_tensor(bias_sum[:, c, :], sc[:, c, 0:KT], bias_in[:, c, :], ALU.add)\
                       .then_inc(bias_ok, 1)
                else:
                    dve.tensor_copy(bias_sum[:, c, :], bias_in[:, c, :]).then_inc(bias_ok, 1)
                if c == 0:
                    dve.wait_ge(bias_ok, place[0] + 1)
                    dve.tensor_scalar(bias_q[:, :], bias_sum[:, 0, :], scale, None, ALU.mult).then_inc(bias_q_ok, 1)

            def row_statistics(blk, t):
                dve.wait_ge(ld_x[t], (blk + 1) * DMA)
                last = dve.bn_stats(stats[:, t, :], x[:, t, :])
                if t == TT - 1:
                    last.then_inc(ln_st, 1)

            def statistics(blk):
                for t in range(TT):
                    row_statistics(blk, t)
                aggregate(blk)

            def aggregate(blk):
                wait_apart(dve, ln_st, blk + 1)
                for t in range(TT):
                    last = dve.bn_aggr(mv[:, t, :], stats[:, t, :])
                last.then_inc(ln_mv, 1)

            def read(item, blk):
                (kind, n, rel), (bank, count) = item
                o = banks[:, bank, :]
                tb = blk + rel
                if kind == "v":
                    return
                dve.wait_ge(done, count)
                if kind in "xe":
                    hi, lo, hi_ok, lo_ok = (xt_h, xt_l, x_hi, x_lo) if kind == "x" else (et_h, et_l, e_hi, e_lo)
                    rows_ = slice(n * P, (n + 1) * P)
                    dve.wait_ge(hi_ok, tb * TT + (n + 1))
                    dve.tensor_tensor(lo[:, :, rows_], o.rearrange("p (f c) -> p f c", f=KT), f32(hi[:, :, rows_]),
                                      ALU.subtract).then_inc(lo_ok, 1)
                elif kind in "qk":
                    hi, lo, bias, hi_ok, lo_ok = (q_h, q_l, bias_q, q_hi, q_lo) if kind == "q" else \
                        (k_h, k_l, bias_sum[:, 1, :], k_hi, k_lo)
                    dve.wait_ge(hi_ok, tb * KT + (n + 1))
                    dve.scalar_tensor_tensor(lo[:, n, :], o, bias[:, n:n + 1], f32(hi[:, n, :]), ALU.add, ALU.subtract)\
                       .then_inc(lo_ok, 1)
                else:
                    dve.wait_ge(res_ok, tb * TT + (n + 1))
                    dve.tensor_tensor(res[:, n % 2, :], o, res[:, n % 2, :], ALU.add).then_inc(y_ok, 1)

            def mask_scores(blk, g, first):
                b = g // KT
                grp = blk * NG + g
                if cross:
                    dve.wait_ge(m_ok, blk * BPB + (b + 1))
                elif first:
                    dve.wait_ge(m_ok, 1)
                dve.wait_ge(scored, grp + 1)
                m = mk[:, b % n_mask, :, :].rearrange("p t s -> p (t s)").unsqueeze(1).to_broadcast([P, HPG, TPB * S])
                dve.tensor_tensor(p[:, g % 2, :, :, :].rearrange("p j t s -> p j (t s)"), sc[:, :, :], m, ALU.mult)\
                   .then_inc(masked, 1)
                dve.wait_ge(masked, grp + 1)

            def maxima(blk, g, j):
                b = g // KT
                for t in range(TPB):
                    a_ = p[:, g % 2, j, t, :]
                    dve.tensor_tensor_reduce(out=a_, in0=a_, in1=ma[:, b % n_mask, t, :], scale=-1.0, scalar=BIG,
                                             op0=ALU.add, op1=ALU.min, accum_out=nmax[:, g % 2, j, t:t + 1])\
                       .then_inc(biased, 1)

            def inverses(blk, g):
                grp = blk * NG + g
                dve.wait_ge(exped, (grp + 1) * HPG * TPB)
                dve.reciprocal(rinv[:, g % 2, :, :], rsum[:, g % 2, :, :]).then_inc(inv_ok, 1)
                dve.wait_ge(inv_ok, grp + 1)
                for t in range(TPB):
                    last = dve.tensor_copy(rwide[:, g % 2, t, :].rearrange("p (j d) -> p j d", j=HPG),
                                           rinv[:, g % 2, :, t:t + 1].to_broadcast([P, HPG, HD]))
                last.then_inc(wide_ok, 1)

            def weighed(blk, g, pv):
                b, f = g // KT, g % KT
                grp = blk * NG + g
                bank, count = pv
                dve.wait_ge(rt_ok, grp + 1)
                wait(dve, c_hi, grp)
                dve.tensor_tensor(cx[:, :], banks[:, bank, 0:S], rt[:, :], ALU.mult).then_inc(cx_ok, 1)
                dve.wait_ge(c_hi, grp + 1)
                cols = slice(b * S, (b + 1) * S)
                dve.scalar_tensor_tensor(ct_l[:, f, cols], cx[:, :], bias_sum[:, 2, f:f + 1], f32(ct_h[:, f, cols]),
                                         ALU.add, ALU.subtract).then_inc(c_lo, 1)

            def normalise(blk, t):
                if t == 0:
                    dve.wait_ge(ln_rs, blk + 1)
                dve.tensor_scalar(x[:, t, :], x[:, t, :], mv[:, t, 0:1], rstd[:, t:t + 1],
                                  ALU.subtract, ALU.mult).then_inc(ln_x, 1)

            def normalise_all():
                for t in range(TT):
                    normalise(0, t)

            def first_maxima():
                dve.wait_ge(w_lo, 4 * KT)
                for j in range(HPG):
                    maxima(0, 0, j)
            before = {"statistics": lambda: statistics(0), "normalise": normalise_all, "unit": lambda item: read(item, -1),
                      "split": split_weights, "bias": biases_of, "scores": lambda: mask_scores(0, 0, True),
                      "maxima": first_maxima}

            def slot(blk, g, first, last, pre, pv, post):
                pb, pg = (blk, g - 1) if g else (blk - 1, NG - 1)
                for item in pre:
                    read(item, blk)
                if g == 1 and not last:
                    normalise(blk + 1, 0)
                    normalise(blk + 1, 1)
                nb, ng = (blk, g + 1) if g + 1 < NG else (blk + 1, 0)
                more = g + 1 < NG or not last
                if more:
                    mask_scores(nb, ng, False)
                if pv is not None:
                    weighed(pb, pg, pv)
                inverses(blk, g)
                post = [item for item in post if item[0][0] != "v"]
                for j in range(HPG):
                    for n, item in enumerate(post):
                        if j == n * HPG // len(post):
                            read(item, blk)
                    if more:
                        maxima(nb, ng, j)
                    if g == 0 and not last:
                        row_statistics(blk + 1, j)
                    if g == 1 and not last and j < 2:
                        normalise(blk + 1, j + 2)
                if g == 0 and not last:
                    aggregate(blk + 1)

            def after(pv, items):
                weighed(NB - 1, NG - 1, pv)
                for item in items:
                    read(item, NB)
            phase(dve, before, slot, after)


def mlp_phase(nc, rows, w1, b1, w2, b2, ln_s, ln_b, m2t_dram, cb_dram, out):
    with ExitStack() as stack:
        r = Room(nc, stack, "M")
        ident = r.sb("ident", [P, P])
        w1_h = r.sb("w1_h", [P, KT, FF], F32R)
        w1_l = r.sb("w1_l", [P, KT, FF], F32R)
        w2_h = r.sb("w2_h", [P, FT, H], F32R)
        w2_l = r.sb("w2_l", [P, FT, H], F32R)
        ln_scale = r.sb("ln_scale", [P, H])
        ln_shift = r.sb("ln_shift", [P, H])
        b1_col = r.sb("b1_col", [P, FT])
        b2_row = r.sb("b2_row", [P, H])
        half = r.sb("half", [P, TT])
        eps = r.sb("eps", [P, TT])
        x = r.sb("x", [P, TT, H])
        stats = r.sb("stats", [P, TT, 6])
        mv = r.sb("mv", [P, TT, 2])
        ve = r.sb("ve", [P, TT])
        rstd = r.sb("rstd", [P, TT])
        xt_h = r.sb("xt_h", [P, KT, TOK], F32R)
        xt_l = r.sb("xt_l", [P, KT, TOK], F32R)
        hf = r.sb("hf", [P, 2, TOK])
        h_h = r.sb("h_h", [P, 2, TOK], F32R)
        h_l = r.sb("h_l", [P, 2, TOK], F32R)
        t_sb = r.sb("t_sb", [P, TT, H])
        t_h = r.sb("t_h", [P, TPB, H], F32R)
        t_l = r.sb("t_l", [P, TPB, H], F32R)
        m2 = r.sb("m2", [P, TPB * S])
        m2_h = r.sb("m2_h", [P, TPB * S], F32R)
        m2_l = r.sb("m2_l", [P, TPB * S], F32R)
        cb = r.sb("cb", [P, BPB, TPB])
        y = r.sb("y", [P, 2, H])
        acc = r.ps("acc", [P, TT, 512])
        hb = r.ps("hb", [P, 2, 512])
        banks = r.ps("banks", [P, 2, 512])

        made, half_ok = r.sem("made"), r.sem("half_ok")
        ld_c, ld_ln = r.sem("ld_c"), r.sem("ld_ln")
        ld_w, ld_x, ld_t, ld_m = r.sems("ld_w", 4), r.sems("ld_x", TT), r.sems("ld_t", TT), r.sem("ld_m")
        ld_b = r.sems("ld_b", BPB)
        ld_m_end = r.sem("ld_m_end")
        st_y = r.sems("st_y", 2)
        w_hi, w_lo, w_lo0 = r.sem("w_hi"), r.sem("w_lo"), r.sem("w_lo0")
        ln_st, ln_mv, ln_ve, ln_rs = (r.sem(f"ln_{n}") for n in ("st", "mv", "ve", "rs"))
        ln_n, ln_g, ln_x = (r.sem(f"ln_{n}") for n in ("n", "g", "x"))
        x_g = r.sem("x_g")
        done, x_hi, x_lo = r.sem("done"), r.sem("x_hi"), r.sem("x_lo")
        h_done, h_act, h_hi, h_lo = (r.sem(n) for n in ("h_done", "h_act", "h_hi", "h_lo"))
        a_done, t_bias, t_ok = r.sem("a_done"), r.sem("t_bias"), r.sem("t_ok")
        t_hi, t_lo, m2_hi, m2_lo, y_ok = (r.sem(n) for n in ("t_hi", "t_lo", "m2_hi", "m2_lo", "y_ok"))
        block = r.block()

        xd = rows.rearrange("b (t p) n -> (b t) p n", p=P)
        yd = out.rearrange("b (t p) n -> (b t) p n", p=P)
        n_consts = 2

        first_chunks = [(1, t, 0) for t in range(KT)]
        slot_chunks = [[(2, f, 0)] + ([(1, f % KT, f // KT + 1)] if f // KT + 1 < KT else []) for f in range(FT)]
        chunks = first_chunks + [c for s in slot_chunks for c in s]
        number = {c: n for n, c in enumerate(chunks)}

        def split(n):
            return (w_lo0, n + 1) if n < len(first_chunks) else (w_lo, n + 1 - len(first_chunks))

        def operands(b, end=False):
            whole = t_sb[:, b * TPB:(b + 1) * TPB, :]
            if end and b == BPB - 1:
                return whole, x[:, 0, :], xt_h[:, 0:TPB, :], xt_l[:, 0:TPB, :], xt_h[:, TPB, :], xt_l[:, TPB, :]
            return whole, m2[:, :], t_h[:, :, :], t_l[:, :, :], m2_h[:, :], m2_l[:, :]

        def parts_of(c):
            m, t, quarter = c
            cols = slice(quarter * 512, (quarter + 1) * 512)
            return (w1_h[:, t, cols], w1_l[:, t, cols]) if m == 1 else (w2_h[:, t, :], w2_l[:, t, :])

        AT = {3: (0, 0), 4: (0, 1), 9: (1, 0), 10: (1, 1)}
        TURNS = [("x", t, 1) for t in range(TT)]

        def read_out(unit, blk):
            kind, n, rel = unit
            if kind == "x":
                return x_lo, (blk + rel) * TT + (n + 1)
            return y_ok, (blk + rel + 1) * TT + (n[0] * TPB + n[1] + 1)

        def phase(eng, before, slot, after):
            units = Units()
            before([(u, units.take()) for u in TURNS])

            def body(blk, first, last):
                for f in range(FT):
                    unit = (("p", AT[f], -1), units.take()) if f in AT and not first else None
                    turns = [(u, units.take()) for u in TURNS] if f == FT - 1 and not last else []
                    slot(blk, f, first, last, unit, turns)
            body(0, True, False)
            with eng.Fori(1, NB - 1) as i:
                units.enter(i - 1, len(AT) + TT)
                body(i, False, False)
            units.leave(NB - 2)
            body(NB - 1, False, True)
            after([(("p", AT[f], -1), units.take()) for f in sorted(AT)])

        @block.sync
        def _(sp):
            def load_chunk(n):
                m, t, quarter = chunks[n]
                if n >= 4:
                    sp.wait_ge(*split(n - 4))
                src = w1[t * P:(t + 1) * P, quarter * 512:(quarter + 1) * 512] if m == 1 else w2[t * P:(t + 1) * P, :]
                sp.dma_start(t_sb[:, n % 4, :], src).then_inc(ld_w[n % 4], DMA)

            def load_rows(blk, first):
                for t in range(TT):
                    if not first:
                        sp.wait_ge(x_lo, (blk - 1) * TT + (t + 1))
                    sp.dma_start(x[:, t, :], xd[blk * TT + t]).then_inc(ld_x[t], DMA)

            def load_t(blk, t):
                sp.dma_start(t_sb[:, t, :], xd[blk * TT + t]).then_inc(ld_t[t], DMA)

            def load_m2(blk, b):
                if isinstance(blk, int) and blk * BPB + b == B - 1:
                    sp.wait_ge(x_lo, NB * TT)
                    sp.dma_start(operands(b, True)[1], m2t_dram[B - 1]).then_inc(ld_m_end, DMA)
                else:
                    sp.wait_ge(m2_lo, blk * BPB + (b + 1))
                    sp.dma_start(m2[:, :], m2t_dram[blk * BPB + b]).then_inc(ld_m, DMA)
                sp.wait_ge(y_ok, blk * TT + (b + 1) * TPB)
                sp.dma_start(cb[:, b, :], cb_dram[blk * BPB + b]).then_inc(ld_b[b], DMA)

            def store(blk, b, t):
                sp.wait_ge(y_ok, (blk + 1) * TT + (b * TPB + t + 1))
                sp.dma_start(yd[blk * TT + (b * TPB + t)], y[:, t, :]).then_inc(st_y[t], DMA)

            for n in range(2):
                sp.sem_inc(st_y[n], DMA)
            load_rows(0, True)
            for dst, src in ((ln_scale, across(ln_s)), (ln_shift, across(ln_b))):
                sp.dma_start(dst[:, :], src).then_inc(ld_ln, DMA)
            for n in range(4):
                load_chunk(n)
            for dst, src in ((b1_col, column(b1)), (b2_row, across(b2))):
                sp.dma_start(dst[:, :], src, allow_slow_non_contiguous=True).then_inc(ld_c, DMA)
            load_rows(1, False)
            for n in range(4, len(chunks)):
                load_chunk(n)
            sp.wait_ge(*split(len(chunks) - 1))
            for t in range(TT):
                load_t(0, t)

            def body(blk, last):
                if not last:
                    load_rows(blk + 1, False)
                load_m2(blk - 1, 0)
                load_m2(blk - 1, 1)
                for b in range(BPB):
                    for t in range(TPB):
                        store(blk - 1, b, t)
                    for t in range(TPB):
                        load_t(blk, b * TPB + t)
            with sp.Fori(1, NB - 1) as i:
                body(i, False)
            body(NB - 1, True)
            load_m2(NB - 1, 0)
            load_m2(NB - 1, 1)
            for b in range(BPB):
                for t in range(TPB):
                    store(NB - 1, b, t)
            for n in range(2):
                sp.wait_ge(st_y[n], DMA * (B * TPB // 2 + 1))

        @block.gpsimd
        def _(pool):
            def deviations(blk):
                pool.wait_ge(ln_mv, blk + 1)
                pool.tensor_tensor(ve[:, :], mv[:, :, 1], eps[:, :], ALU.add).then_inc(ln_ve, 1)
                pool.wait_ge(ln_ve, blk + 1)
                pool.tensor_tensor(rstd[:, :], ve[:, :], half[:, :], ALU.pow).then_inc(ln_rs, 1)

            def normalise(blk):
                deviations(blk)
                wait_apart(pool, ln_rs, blk + 1)
                for t in range(TT):
                    pool.tensor_scalar(x[:, t, :], x[:, t, :], mv[:, t, 0:1], rstd[:, t:t + 1],
                                       ALU.subtract, ALU.mult).then_inc(ln_n, 1)
                    pool.wait_ge(ln_n, (blk - 1) * TT + (t + 1))
                    pool.tensor_tensor(x[:, t, :], x[:, t, :], ln_scale[:, :], ALU.mult).then_inc(ln_g, 1)
                    pool.wait_ge(ln_g, (blk - 1) * TT + (t + 1))
                    pool.tensor_tensor(x[:, t, :], x[:, t, :], ln_shift[:, :], ALU.add).then_inc(ln_x, 1)

            def add_bias(blk):
                for t in range(TT):
                    pool.wait_ge(ld_t[t], (blk + 1) * DMA)
                    pool.tensor_tensor(t_sb[:, t, :], t_sb[:, t, :], b2_row[:, :], ALU.add).then_inc(t_bias, 1)

            make_identity(pool, ident, made)
            pool.memset(half[:, :], -0.5).then_inc(half_ok, 1)
            pool.memset(eps[:, :], EPS).then_inc(half_ok, 1)
            pool.wait_ge(half_ok, 2)
            deviations(0)
            for n in range(len(first_chunks)):
                hi, lo = parts_of(chunks[n])
                pool.wait_ge(w_hi, n + 1)
                pool.tensor_tensor(lo, t_sb[:, n, :], f32(hi), ALU.subtract).then_inc(w_lo0, 1)
            pool.wait_ge(ld_ln, 2 * DMA)
            pool.wait_ge(ld_c, n_consts * DMA)
            normalise(1)
            add_bias(0)
            with pool.Fori(1, NB - 1) as i:
                normalise(i + 1)
                add_bias(i)
            add_bias(NB - 1)

        @block.tensor
        def _(pe):
            in_bank = [None, None]

            def occupy(unit, bank, blk):
                if in_bank[bank] is not None:
                    wait(pe, *read_out(in_bank[bank], blk))
                in_bank[bank] = unit

            def older():
                for b in range(2):
                    if in_bank[b] is not None:
                        kind, n, rel = in_bank[b]
                        in_bank[b] = kind, n, rel - 1

            def turn(item, blk):
                unit, (bank, _) = item
                occupy(unit, bank, blk)
                n, tb = unit[1], blk + unit[2]
                pe.wait_ge(ln_x, tb * TT + (n + 1))
                for f in range(KT):
                    last = pe.transpose(banks[:, bank, f * P:(f + 1) * P], x[:, n, f * P:(f + 1) * P], ident[:, :])
                last.then_inc(done, 1)

            def hidden(blk, f, first):
                n = blk * FT + f
                if f == 0:
                    pe.wait_ge(x_lo, (blk + 1) * TT)
                if first and f % KT == 0:
                    pe.wait_ge(*split(number[(1, KT - 1, f // KT)]))
                wait(pe, h_act, n - 1)
                cols = slice(f * P, (f + 1) * P)
                for t in range(KT):
                    last = product(pe, hb[:, f % 2, :], (w1_h[:, t, cols], w1_l[:, t, cols]),
                                   (xt_h[:, t, :], xt_l[:, t, :]), t == 0, t == KT - 1)
                last.then_inc(h_done, 1)

            def second(blk, f, first):
                if first:
                    pe.wait_ge(*split(number[(2, f, 0)]))
                if f == 0:
                    wait(pe, t_ok, blk * TT)
                pe.wait_ge(h_lo, blk * FT + (f + 1))
                for t in range(TT):
                    rows_ = slice(t * P, (t + 1) * P)
                    last = product(pe, acc[:, t, :], (h_h[:, f % 2, rows_], h_l[:, f % 2, rows_]),
                                   (w2_h[:, f, :], w2_l[:, f, :]), f == 0, f == FT - 1)
                last.then_inc(a_done, 1)

            def last_product(item, blk, end=False):
                unit, (bank, _) = item
                b, o = unit[1]
                tb = blk + unit[2]
                occupy(unit, bank, blk)
                pe.wait_ge(t_lo, tb * BPB + (b + 1))
                pe.wait_ge(m2_lo, tb * BPB + (b + 2))
                _, _, th, tl, mh, ml = operands(b, end)
                for t in range(TPB):
                    cols = slice(t * S + o * P, t * S + (o + 1) * P)
                    last = product(pe, banks[:, bank, :], (mh[:, cols], ml[:, cols]), (th[:, t, :], tl[:, t, :]),
                                   t == 0, t == TPB - 1)
                last.then_inc(done, 1)

            def before(items):
                pe.wait_ge(made, 2)
                for item in items:
                    turn(item, -1)
                older()

            def slot(blk, f, first, last, unit, turns):
                if f == 0 and not first:
                    older()
                hidden(blk, f, first)
                for item in turns[:2]:
                    turn(item, blk)
                if f:
                    second(blk, f - 1, first)
                if unit:
                    last_product(unit, blk)
                if f == FT - 1:
                    for item in turns[2:]:
                        turn(item, blk)
                    second(blk, f, first)

            def after(items):
                older()
                for item in items:
                    last_product(item, NB, True)
            phase(pe, before, slot, after)

        @block.scalar
        def _(act):
            def split_weights(c):
                n = number[c]
                act.wait_ge(ld_w[n % 4], (n // 4 + 1) * DMA)
                act.activation(parts_of(c)[0], t_sb[:, n % 4, :], ACT.Copy).then_inc(w_hi, 1)

            def turned(item, blk):
                (kind, n, rel), (bank, count) = item
                act.wait_ge(done, count)
                act.activation(xt_h[:, :, n * P:(n + 1) * P], banks[:, bank, :].rearrange("p (f c) -> p f c", f=KT),
                               ACT.Copy).then_inc(x_hi, 1)

            def split_t(blk, b, end=False):
                whole, raw, th, _, mh, _ = operands(b, end)
                own = end and b == BPB - 1
                act.wait_ge(t_ok, blk * TT + (b + 1) * TPB)
                if not own:
                    act.wait_ge(y_ok, (blk + 1) * TT + b * TPB)
                act.activation(th, whole, ACT.Copy).then_inc(t_hi, 1)
                act.wait_ge(*((ld_m_end, DMA) if own else (ld_m, (blk * BPB + (b + 1)) * DMA)))
                act.activation(mh, raw, ACT.Copy).then_inc(m2_hi, 1)

            def before(items):
                for c in first_chunks:
                    split_weights(c)
                for item in items:
                    turned(item, -1)
                act.wait_ge(ld_c, n_consts * DMA)

            def slot(blk, f, first, last, unit, turns):
                if first:
                    for c in slot_chunks[f]:
                        split_weights(c)
                n = blk * FT + f
                act.wait_ge(h_done, n + 1)
                wait(act, h_lo, n - 1)
                act.activation(hf[:, f % 2, :], hb[:, f % 2, :], ACT.Gelu_apprx_tanh, bias=b1_col[:, f:f + 1])\
                   .then_inc(h_act, 1)
                if not first and f in (0, 5):
                    split_t(blk - 1, f // 5)
                for item in turns:
                    turned(item, blk)

            def after(items):
                split_t(NB - 1, 0, True)
                split_t(NB - 1, 1, True)
            phase(act, before, slot, after)

        @block.vector
        def _(dve):
            def split_weights(c):
                n = number[c]
                hi, lo = parts_of(c)
                dve.wait_ge(w_hi, n + 1)
                dve.tensor_tensor(lo, t_sb[:, n % 4, :], f32(hi), ALU.subtract).then_inc(w_lo, 1)

            def statistics(blk):
                for t in range(TT):
                    dve.wait_ge(ld_x[t], (blk + 1) * DMA)
                    last = dve.bn_stats(stats[:, t, :], x[:, t, :])
                last.then_inc(ln_st, 1)
                wait_apart(dve, ln_st, blk + 1)
                for t in range(TT):
                    last = dve.bn_aggr(mv[:, t, :], stats[:, t, :])
                last.then_inc(ln_mv, 1)

            def turned(item, blk):
                (kind, n, rel), (bank, count) = item
                rows_ = slice(n * P, (n + 1) * P)
                dve.wait_ge(x_hi, (blk + rel) * TT + (n + 1))
                dve.tensor_tensor(xt_l[:, :, rows_], banks[:, bank, :].rearrange("p (f c) -> p f c", f=KT),
                                  f32(xt_h[:, :, rows_]), ALU.subtract).then_inc(x_lo, 1)

            def split_t(blk, b, end=False):
                whole, raw, th, tl, mh, ml = operands(b, end)
                n = blk * BPB + (b + 1)
                dve.wait_ge(t_hi, n)
                dve.tensor_tensor(tl, whole, f32(th), ALU.subtract).then_inc(t_lo, 1)
                dve.wait_ge(m2_hi, n)
                dve.tensor_tensor(ml, raw, f32(mh), ALU.subtract).then_inc(m2_lo, 1)

            def last_out(item, blk):
                (kind, (b, o), rel), (bank, count) = item
                tb = blk + rel
                dve.wait_ge(done, count)
                dve.wait_ge(ld_b[b], (tb + 1) * DMA)
                dve.wait_ge(st_y[o], (tb * BPB + (b + 1)) * DMA)
                dve.scalar_tensor_tensor(y[:, o, :], banks[:, bank, :], cb[:, b, o:o + 1], t_sb[:, b * TPB + o, :],
                                         ALU.add, ALU.add).then_inc(y_ok, 1)

            def before(items):
                dve.sem_inc(y_ok, TT)
                dve.sem_inc(m2_lo, 1)
                statistics(0)
                dve.wait_ge(ld_ln, 2 * DMA)
                dve.wait_ge(ln_rs, 1)
                for t in range(TT):
                    dve.scalar_tensor_tensor(x[:, t, :], x[:, t, :], mv[:, t, 0:1], ln_scale[:, :],
                                             ALU.subtract, ALU.mult).then_inc(x_g, 1)
                for t in range(TT):
                    dve.wait_ge(x_g, t + 1)
                    dve.scalar_tensor_tensor(x[:, t, :], x[:, t, :], rstd[:, t:t + 1], ln_shift[:, :],
                                             ALU.mult, ALU.add).then_inc(ln_x, 1)
                for item in items:
                    turned(item, -1)
                statistics(1)

            def slot(blk, f, first, last, unit, turns):
                if first:
                    for c in slot_chunks[f]:
                        split_weights(c)
                n = blk * FT + f
                dve.wait_ge(h_act, n + 1)
                if not (first and f < 2):
                    dve.wait_ge(a_done, n - 1)
                dve.tensor_copy(h_h[:, f % 2, :], hf[:, f % 2, :]).then_inc(h_hi, 1)
                dve.wait_ge(h_hi, n + 1)
                dve.tensor_tensor(h_l[:, f % 2, :], hf[:, f % 2, :], f32(h_h[:, f % 2, :]), ALU.subtract)\
                   .then_inc(h_lo, 1)
                if f == 1 and not first and not last:
                    statistics(blk + 1)
                if not first and f in (0, 5):
                    split_t(blk - 1, f // 5)
                if unit:
                    last_out(unit, blk)
                for item in turns:
                    turned(item, blk)
                if f == FT - 1:
                    dve.wait_ge(a_done, n + 1)
                    for t in range(TT):
                        dve.wait_ge(t_bias, blk * TT + (t + 1))
                        dve.tensor_tensor(t_sb[:, t, :], acc[:, t, :], t_sb[:, t, :], ALU.add).then_inc(t_ok, 1)

            def after(items):
                split_t(NB - 1, 0, True)
                split_t(NB - 1, 1, True)
                for item in items:
                    last_out(item, NB)
            phase(dve, before, slot, after)


def decoder_layer_and_nonlocal(nc, a, out):
    m2t = nc.dram_tensor("m2t", [B, P, TPB * S], F32, kind="Internal").ap()
    cb = nc.dram_tensor("cb", [B, P, TPB], F32, kind="Internal").ap()
    x1 = nc.dram_tensor("x1", [B, S, H], F32, kind="Internal").ap()
    x2 = nc.dram_tensor("x2", [B, S, H], F32, kind="Internal").ap()
    nl = {k[len("L1_xattn_"):]: v for k, v in a.items() if k.startswith("L1_xattn_")}
    d = {k[len("L0_xattn_"):]: v for k, v in a.items() if k.startswith("L0_xattn_")}
    context = a["ctx_2048"]
    nonlocal_phase(nc, {**nl, "ctx": context}, m2t, cb)
    attention_phase(nc, "S", a["x"], None, a["mask_1x1xSxS2_fc1"],
                    [d["w_qkv"][:, c * H:(c + 1) * H] for c in range(3)] + [d["w_ao"]],
                    [d["b_qkv"][c * H:(c + 1) * H] for c in range(3)], d["b_ao"], d["ln1_s"], d["ln1_b"], x1)
    attention_phase(nc, "X", x1, context, a["mask_Bx1xSxS2_ff1"],
                    [d["w_q"], d["w_kv"][:, 0:H], d["w_kv"][:, H:2 * H], d["w_co"]],
                    [d["b_q"], d["b_kv"][0:H], d["b_kv"][H:2 * H]], d["b_co"], d["ln2_s"], d["ln2_b"], x2)
    mlp_phase(nc, x2, d["w1"], d["b1"], d["w2"], d["b2"], d["ln3_s"], d["ln3_b"], m2t, cb, out)


def kernel(**inputs):
    import concourse.bacc as bacc
    from concourse.bass_utils import run_bass_kernel_spmd

    nc = bacc.Bacc("TRN2", target_bir_lowering=False, num_devices=1)
    arrays, aps = {}, {}
    for name, value in inputs.items():
        arrays[name] = np.ascontiguousarray(value)
        aps[name] = nc.dram_tensor(name, arrays[name].shape, mybir.dt.from_np(arrays[name].dtype),
                                   kind="ExternalInput").ap()
    out = nc.dram_tensor("out", [B, S, H], F32, kind="ExternalOutput").ap()
    decoder_layer_and_nonlocal(nc, aps, out)
    return run_bass_kernel_spmd(nc, [arrays], core_ids=[0]).results[0]["out"]
```
